# Optimizing a Trainium2 kernel written in Bass

```python
import numpy as np
import jax
import jax.numpy as jnp

def _softmax(x, axis=-1):
    return jax.nn.softmax(x, axis=axis)

def _gelu(x):
    return jax.nn.gelu(x, approximate=True)

def _silu(x):
    return jax.nn.silu(x)

def _sigmoid(x):
    return jax.nn.sigmoid(x)

def _layernorm(x, axis=-1, eps=1e-05):
    m = jnp.mean(x, axis=axis, keepdims=True)
    v = jnp.var(x, axis=axis, keepdims=True)
    return (x - m) / jnp.sqrt(v + eps)

def _scatter_add(tgt, idx, src, axis=0):
    return tgt.at[idx].add(src)

def _segment_sum(src, seg, n):
    return jax.ops.segment_sum(src, seg, n)
kernel_name = 'mk_adj_resnorm_d2_adj_r2_a22813'

def setup_inputs(seed: int=0):
    np.random.seed(seed)
    _w = jnp.asarray

    def _rec_inputs():
        import jax
        import jax.numpy as jnp
        _gk = jax.random.key(seed)
        x = -0.0005963 + 1.001 * jax.random.normal(jax.random.fold_in(_gk, 1), (2048, 256), jnp.float32)
        _a = jax.random.bernoulli(jax.random.fold_in(_gk, 2), 0.00390625, (2048, 2048))
        _af = _a.astype(jnp.float32)
        adj = _af
        return (x, adj)
    x, adj = _rec_inputs()

    def _L0_gnn_setup():
        import jax, jax.numpy as jnp
        import numpy as np
        N = 3072
        D_IN = 256
        D_OUT = 256
        DENSITY = 0.005
        key = jax.random.key(seed)
        ks = jax.random.split(key, 12)
        x = jax.random.normal(ks[0], (N, D_IN), dtype=jnp.float32)
        adj_a = (jax.random.uniform(ks[1], (N, N)) < DENSITY).astype(jnp.float32)
        adj_b = (jax.random.uniform(ks[2], (N, N)) < DENSITY).astype(jnp.float32)
        W_sa = jax.random.normal(ks[3], (D_IN, D_OUT), dtype=jnp.float32) * (1.414 / np.sqrt(D_IN + D_OUT))
        a_sa = jax.random.normal(ks[4], (1, 2 * D_OUT), dtype=jnp.float32) * (1.414 / np.sqrt(1 + 2 * D_OUT))
        stdv = 1.0 / np.sqrt(D_OUT)
        W_gcnb = jax.random.uniform(ks[5], (D_IN, D_OUT), minval=-stdv, maxval=stdv, dtype=jnp.float32)
        b_gcnb = jax.random.uniform(ks[6], (D_OUT,), minval=-stdv, maxval=stdv, dtype=jnp.float32)
        s = 1.0 / np.sqrt(2 * D_IN)
        Wa = jax.random.uniform(ks[7], (1, 2 * D_IN), minval=-s, maxval=s, dtype=jnp.float32)
        ba = jax.random.uniform(ks[8], (1,), minval=-s, maxval=s, dtype=jnp.float32)
        Wb = jax.random.uniform(ks[9], (1, 2 * D_IN), minval=-s, maxval=s, dtype=jnp.float32)
        bb = jax.random.uniform(ks[10], (1,), minval=-s, maxval=s, dtype=jnp.float32)
        return {'x': x, 'adj_a': adj_a, 'adj_b': adj_b, 'W_sa': W_sa, 'a_sa': a_sa, 'W_gcnb': W_gcnb, 'b_gcnb': b_gcnb, 'Wa': Wa, 'ba': ba, 'Wb': Wb, 'bb': bb}
    _L0_gnn_all = _L0_gnn_setup()
    _L0_gnn_in = {k: v for k, v in _L0_gnn_all.items() if k in ('W_sa', 'a_sa', 'W_gcnb', 'b_gcnb', 'Wa', 'ba', 'Wb', 'bb')}
    del _L0_gnn_all

    def _L1_gnn_setup():
        import jax, jax.numpy as jnp
        import numpy as np
        N = 1024
        HID = 256
        H = 8
        key = jax.random.key(seed)
        ks = jax.random.split(key, 8)
        x = jax.random.normal(ks[0], (N, HID), dtype=jnp.float32)
        sp = jax.random.normal(ks[1], (N, N), dtype=jnp.float32)
        zero_mask = jax.random.uniform(ks[2], (N, N)) < 0.2
        spatial_encoding = jnp.where(zero_mask, 0.0, sp)
        edge_encoding = jax.random.normal(ks[3], (N, N), dtype=jnp.float32)
        s = 1.0 / np.sqrt(HID)
        Wq = jax.random.normal(ks[4], (HID, HID * H), dtype=jnp.float32) * s
        Wk = jax.random.normal(ks[5], (HID, HID * H), dtype=jnp.float32) * s
        Wv = jax.random.normal(ks[6], (HID, HID * H), dtype=jnp.float32) * s
        Wout = jax.random.normal(ks[7], (HID * H, HID), dtype=jnp.float32) * (1.0 / np.sqrt(HID * H))
        return {'x': x, 'spatial_encoding': spatial_encoding, 'edge_encoding': edge_encoding, 'Wq': Wq, 'Wk': Wk, 'Wv': Wv, 'Wout': Wout}
    _L1_gnn_all = _L1_gnn_setup()
    _L1_gnn_in = {k: v for k, v in _L1_gnn_all.items() if k in ('Wq', 'Wk', 'Wv', 'Wout')}
    del _L1_gnn_all
    return {'x': x, 'adj': adj, 'L0_gnn_W_sa': _L0_gnn_in['W_sa'], 'L0_gnn_a_sa': _L0_gnn_in['a_sa'], 'L0_gnn_W_gcnb': _L0_gnn_in['W_gcnb'], 'L0_gnn_b_gcnb': _L0_gnn_in['b_gcnb'], 'L0_gnn_Wa': _L0_gnn_in['Wa'], 'L0_gnn_ba': _L0_gnn_in['ba'], 'L0_gnn_Wb': _L0_gnn_in['Wb'], 'L0_gnn_bb': _L0_gnn_in['bb'], 'L1_gnn_Wq': _L1_gnn_in['Wq'], 'L1_gnn_Wk': _L1_gnn_in['Wk'], 'L1_gnn_Wv': _L1_gnn_in['Wv'], 'L1_gnn_Wout': _L1_gnn_in['Wout']}

def reference(x, adj, L0_gnn_W_sa, L0_gnn_a_sa, L0_gnn_W_gcnb, L0_gnn_b_gcnb, L0_gnn_Wa, L0_gnn_ba, L0_gnn_Wb, L0_gnn_bb, L1_gnn_Wq, L1_gnn_Wk, L1_gnn_Wv, L1_gnn_Wout):
    import jax
    import jax.numpy as jnp

    def _L0_gnn_ref(x, adj_a, adj_b, W_sa, a_sa, W_gcnb, b_gcnb, Wa, ba, Wb, bb):
        import jax, jax.numpy as jnp
        import numpy as np
        N = 3072
        D_IN = 256
        D_OUT = 256
        DENSITY = 0.005
        type_sum_a = adj_a @ x
        type_sum_b = adj_b @ x
        attn_a = jax.nn.sigmoid(jnp.concatenate([type_sum_a, x], axis=1) @ Wa.T + ba)
        attn_b = jax.nn.sigmoid(jnp.concatenate([type_sum_b, x], axis=1) @ Wb.T + bb)
        h = x @ W_sa
        Hd = h.shape[1]
        s_left = h @ a_sa[0, :Hd]
        s_right = h @ a_sa[0, Hd:]
        scores = s_left[:, None] + s_right[None, :]
        e = jnp.where(adj_a != 0, jnp.exp(-jax.nn.leaky_relu(scores, 0.01)), 0.0)
        attn = e / (jnp.sum(e, axis=1, keepdims=True) + 1e-05)
        x_a = attn @ h
        x_b = adj_b @ (x @ W_gcnb) + b_gcnb
        return jax.nn.sigmoid(attn_a * x_a + attn_b * x_b)

    def _L1_gnn_ref(x, spatial_encoding, edge_encoding, Wq, Wk, Wv, Wout):
        import jax, jax.numpy as jnp
        import numpy as np
        N = 1024
        HID = 256
        H = 8
        n, d = x.shape
        h = Wq.shape[1] // d
        scale = d ** (-0.5)
        q = (x @ Wq).reshape(h, n, d)
        k = (x @ Wk).reshape(h, n, d)
        v = (x @ Wv).reshape(h, n, d)
        a = jnp.einsum('hnd,hmd->hnm', q, k) * scale
        a = a + spatial_encoding + edge_encoding
        mask = spatial_encoding == 0.0
        a = jnp.where(mask, -1000000.0, a)
        a = jax.nn.softmax(a, axis=-1)
        a = jnp.where(mask, 0.0, a)
        out = jnp.einsum('hnm,hmd->hnd', a, v)
        out = out.transpose(1, 0, 2).reshape(n, h * d)
        return out @ Wout
    x = _layernorm(x + _L0_gnn_ref(x, adj, adj, L0_gnn_W_sa, L0_gnn_a_sa, L0_gnn_W_gcnb, L0_gnn_b_gcnb, L0_gnn_Wa, L0_gnn_ba, L0_gnn_Wb, L0_gnn_bb), axis=-1)
    x = _layernorm(x + _L1_gnn_ref(x, adj, adj, L1_gnn_Wq, L1_gnn_Wk, L1_gnn_Wv, L1_gnn_Wout), axis=-1)
    return x

_drawn_inputs = setup_inputs


def setup_inputs(seed=0):
    import zlib

    import numpy as np

    out = dict(_drawn_inputs(seed))
    spreads = {}
    factors = {'L0_gnn_b_gcnb': 8.0}
    for name, (base, spread) in spreads.items():
        noise = np.random.default_rng([zlib.crc32(name.encode()), seed]).standard_normal(out[name].shape)
        drawn = base * np.exp(spread * noise) if base else spread * noise
        out[name] = jnp.asarray(drawn.astype(out[name].dtype))
    for name, factor in factors.items():
        out[name] = (out[name] * factor).astype(out[name].dtype)
    return out
```

```python
import concourse.bass as bass
from concourse import mybir
from contextlib import ExitStack

P = 128
BANK = 512
BIG = float(2 ** 100)
REF_MASK = -1.0e6
LOWEST = -3.0e38


def gnn_two_layers(nc, x, adj, w_sa, a_sa, w_gcnb, b_gcnb, wa, ba, wb, bb, wq, wk, wv, wout, out):
    f32, f32r = mybir.dt.float32, mybir.dt.float32r
    ALU, ACT, AX = mybir.AluOpType, mybir.ActivationFunctionType, mybir.AxisListType

    N, D = x.shape
    HEADS = wq.shape[1] // D
    C = HEADS
    R = N // C
    KT = D // P
    RC = R // P
    NT = N // P
    QCH = N // BANK
    LN_EPS = 1e-5

    bias_d = nc.dram_tensor("bias_scratch", (NT, P, N), f32, kind="Internal").ap()
    x1_d = nc.dram_tensor("x1_scratch", (P, NT * D), f32, kind="Internal").ap()
    x1t_d = nc.dram_tensor("x1t_scratch", (P, KT, N), f32, kind="Internal").ap()

    whole = ExitStack()
    with whole:
        bank = [whole.enter_context(nc.psum_tensor(f"bank{i}", [P, BANK], f32)) for i in range(8)]

        def keep(name, shape, dt=f32):
            return whole.enter_context(nc.sbuf_tensor(name, shape, dt))

        ident = keep("ident", [P, P])
        masked_count = keep("masked_count", [P, NT])
        layer0(nc, locals())
        layer1(nc, locals())




def layer0(nc, g):
    f32, f32r, ALU, ACT = g["f32"], g["f32r"], g["ALU"], g["ACT"]
    N, D, C, RC, KT, NT, QCH = (g[k] for k in ("N", "D", "C", "RC", "KT", "NT", "QCH"))
    bank, ident, masked_count = g["bank"], g["ident"], g["masked_count"]
    GW = D + 2
    HW = D + 1
    RING = 3
    JP = NT // 2
    STEPS = 2 * JP
    IB = RC * P

    ctx = ExitStack()
    with ctx:
        def sb(name, shape, dt=f32):
            return ctx.enter_context(nc.sbuf_tensor("l0_" + name, shape, dt))

        def sem(name):
            return ctx.enter_context(nc.semaphore("l0_" + name))

        xn = sb("xn", [P, RC, C, D])
        xt = sb("xt", [P, KT, N])
        proj = sb("proj", [P, KT, GW + HW])
        gate_x = sb("gate_x", [P, KT, 2])
        a_bc = sb("a_bc", [P, 2 * D])
        wl = sb("wl", [P, KT, 1])
        wl_rep = sb("wl_rep", [P, KT, P])
        ones = sb("ones", [P, P])
        b_bc = sb("b_bc", [P, D])
        gate_b = sb("gate_b", [P, 2])
        junk = sb("junk", [P, D])
        g_hi, g_lo = sb("g_hi", [P, NT, GW], f32r), sb("g_lo", [P, NT, GW], f32r)
        h_hi, h_lo = sb("h_hi", [P, NT, GW], f32r), sb("h_lo", [P, NT, GW], f32r)
        s_right = sb("s_right", [P, NT])
        s_left = sb("s_left", [P, C, RC, P])
        gate_xi = sb("gate_xi", [P, NT, 2])
        adj_n = [sb(f"adj_n{i}", [P, RC, N]) for i in range(2)]
        at_hi, at_lo = ([sb(f"at_{w}{i}", [P, 2, IB], f32r) for i in range(RING)] for w in ("hi", "lo"))
        et_hi, et_lo = ([sb(f"et_{w}{i}", [P, 2, IB], f32r) for i in range(RING)] for w in ("hi", "lo"))
        off = sb("off", [P, 2, IB])
        z = sb("z", [P, 2, IB])
        leaky = [sb(f"leaky{i}", [P, 2, IB]) for i in range(2)]
        e32 = leaky
        bias_t = [sb(f"bias_t{i}", [P, C, N // C]) for i in range(2)]
        count_junk = sb("count_junk", [P, N], mybir.dt.uint8)
        pg, ph = sb("pg", [P, RC, GW]), sb("ph", [P, RC, GW])
        gates = sb("gates", [P, 3, RC, 2])
        den = sb("den", [P, 2, RC])
        mix = sb("mix", [P, 2, RC, D])
        stats = sb("stats", [P, RC, 6])
        moments = sb("moments", [P, RC, 2])
        mv = sb("mv", [P, NT, 2])
        rstd = sb("rstd", [P, 3, NT])
        eps = sb("eps", [P, 1])

        pool_tick, dve_tick, sp_tick = sem("pool_tick"), sem("dve_tick"), sem("sp_tick")
        ident_ready, in_x, in_w, in_small = sem("ident_ready"), sem("in_x"), sem("in_w"), sem("in_small")
        wl_ready, wl_done = sem("wl_ready"), sem("wl_done")
        slot_full, slot_hi, slot_free = sem("slot_full"), sem("slot_hi"), sem("slot_free")
        adj_in = [sem(f"adj_in{i}") for i in range(2)]
        t_full, at_hi_ready, t_free = sem("t_full"), sem("at_hi_ready"), sem("t_free")
        z_ready, leaky_ready, e_ready, et_hi_ready, et_lo_ready = (
            sem("z_ready"), sem("leaky_ready"), sem("e_ready"), sem("et_hi_ready"), sem("et_lo_ready"))
        g_done, h_done = sem("g_done"), sem("h_done")
        pg_copied, ph_copied = sem("pg_copied"), sem("ph_copied")
        counted, masked_dve, masked_off, bias_built = sem("counted"), sem("masked_dve"), sem("masked_off"), sem("bias_built")
        bias_stored = [sem(f"bias_stored{i}") for i in range(2)]
        mixed, gate_exp, mix_exp = sem("mixed"), sem("gate_exp"), sem("mix_exp")
        std_ready, rstd_step, x1_ready, x1t_full, x1t_ready, stored = (
            sem("std_ready"), sem("rstd_step"), sem("x1_ready"), sem("x1t_full"), sem("x1t_ready"), sem("stored"))

        adj_v = g["adj"].rearrange("(rc p c) m -> c p rc m", rc=RC, p=P)
        XT_SLOTS = KT * RC * 2
        PROJ0 = XT_SLOTS
        LEFT0 = PROJ0 + 2 * NT
        GATE0 = LEFT0 + QCH
        SLOTS = GATE0 + 1
        slot_bank = [bank[4 + i % 4] for i in range(SLOTS)]
        LINKS = 16

        def xt_dst(t, kt, rc, ch):
            v = t[:, kt, rc * P * C:(rc + 1) * P * C].rearrange("x (p c) -> x c p", c=C)
            return v[:, 4 * ch:4 * ch + 4, :]

        block = ctx.enter_context(nc.Block())

        @block.sync
        def _(sp):
            sp.dma_start(xn[:], g["x"].rearrange("(rc p c) d -> p rc c d", rc=RC, p=P)).then_inc(in_x, 16)
            sp.dma_start(proj[:, :, 0:D], g["w_gcnb"].rearrange("(k p) n -> p k n", p=P)).then_inc(in_w, 16)
            sp.dma_start(proj[:, :, GW:GW + D], g["w_sa"].rearrange("(k p) n -> p k n", p=P)).then_inc(in_w, 16)
            sp.dma_start(a_bc[:], g["a_sa"].partition_broadcast(P)).then_inc(in_small, 16)
            for i, w in enumerate((g["wa"], g["wb"])):
                col = w.rearrange("o (s k p) -> p s k o", s=2, p=P)
                sp.dma_start(proj[:, :, D + i:D + i + 1], col[:, 0], allow_slow_non_contiguous=True).then_inc(in_small, 16)
                sp.dma_start(gate_x[:, :, i:i + 1], col[:, 1], allow_slow_non_contiguous=True).then_inc(in_small, 16)
            sp.dma_start(b_bc[:], g["b_gcnb"].partition_broadcast(P)).then_inc(in_small, 16)
            for i, b in enumerate((g["ba"], g["bb"])):
                sp.dma_start(gate_b[:, i:i + 1], b.partition_broadcast(P)).then_inc(in_small, 16)
            sp.dma_start(adj_n[0][:], adj_v[0]).then_inc(adj_in[0], 16)
            sp.dma_start(adj_n[1][:], adj_v[1]).then_inc(adj_in[1], 16)
            with sp.Fori(0, C // 2 - 1) as it:
                for par in range(2):
                    sp.wait_ge(t_full, it * STEPS + (par + 1) * JP)
                    sp.sem_inc(sp_tick)
                    sp.wait_ge(counted, it * 2 + par + 1)
                    sp.sem_inc(sp_tick)
                    sp.wait_ge(bias_built, it * 2 * RC + (par + 1) * RC)
                    sp.sem_inc(sp_tick)
                    sp.dma_start(adj_n[par][:], adj_v[bass.ds(it * 2 + 2 + par, 1)].rearrange(
                        "o p rc m -> (o p) rc m")).then_inc(adj_in[par], 16)
            sp.wait_ge(x1_ready, NT)
            sp.dma_start(g["x1_d"], xn[:].rearrange("p r c d -> p (r c d)")).then_inc(stored, 16)
            sp.wait_ge(x1t_ready, XT_SLOTS)
            sp.dma_start(g["x1t_d"], xt[:]).then_inc(stored, 16)
            sp.wait_ge(stored, 32)

        @block.gpsimd
        def _(pool):
            nc.gpsimd.memset(ident[:], 0.0).then_inc(ident_ready, 1)
            pool.wait_ge(ident_ready, 1)
            nc.gpsimd.affine_select(out=ident[:], in_=ident[:], compare_op=ALU.not_equal, fill=1.0, base=0,
                                    pattern=[[-1, P]], channel_multiplier=1).then_inc(ident_ready, 1)
            with pool.Fori(0, C // 2) as it:
                for par in range(2):
                    pool.wait_ge(adj_in[par], it * 16 + 16)
                    for rc in range(RC):
                        tile = it * 2 * RC + par * RC + rc
                        src = adj_n[par][:, rc, :].rearrange("p (r c) -> p c r", c=C)
                        if par:
                            pool.wait_ge(bias_stored[rc], it * 32 + 16)
                        pool.sem_inc(pool_tick)
                        nc.gpsimd.tensor_scalar(bias_t[rc][:], src, 0.0, -BIG, ALU.is_equal,
                                                ALU.mult).then_inc(masked_off, 1)
                        pool.wait_ge(masked_off, tile + 1)
                        nc.gpsimd.tensor_tensor(bias_t[rc][:], bias_t[rc][:], src, ALU.add).then_inc(bias_built, 1)
                        pool.wait_ge(bias_built, tile + 1)
                        pool.sem_inc(pool_tick)
                        pool.dma_start(g["bias_d"][bass.ds(tile, 1)].rearrange("o p n -> (o p) n"),
                                       bias_t[rc][:].rearrange("p c r -> p (c r)")).then_inc(bias_stored[rc], 16)
                for rc in range(RC):
                    pool.wait_ge(bias_stored[rc], it * 32 + 32)

        @block.tensor
        def _(pe):
            pe.wait_ge(ident_ready, 2)
            pe.wait_ge(in_x, 16)
            slot = 0

            def take():
                nonlocal slot
                if slot >= 4:
                    pe.wait_ge(slot_free, slot - 3)
                slot += 1
                return slot_bank[slot - 1]

            for kt in range(KT):
                for rc in range(RC):
                    for ch in range(2):
                        b = take()
                        for i in range(4):
                            last = nc.tensor.transpose(b[:, i * P:(i + 1) * P], xn[:, rc, 4 * ch + i, kt * P:(kt + 1) * P], ident[:])
                        last.then_inc(slot_full, 1)
            pe.wait_ge(slot_free, XT_SLOTS)
            pe.wait_ge(in_w, 32)
            pe.wait_ge(in_small, 128)
            pe.wait_ge(wl_ready, 4)
            for j in range(NT):
                for o, w in ((0, GW), (GW, HW)):
                    b = take()
                    for kt in range(KT):
                        last = nc.tensor.matmul(b[:, 0:w], xt[:, kt, j * P:(j + 1) * P], proj[:, kt, o:o + w],
                                                start=kt == 0, stop=kt == KT - 1)
                    last.then_inc(slot_full, 1)
            pe.wait_ge(wl_done, KT)
            for q in range(QCH):
                b = take()
                for kt in range(KT):
                    last = nc.tensor.matmul(b[:], wl_rep[:, kt, :], xt[:, kt, q * BANK:(q + 1) * BANK],
                                            start=kt == 0, stop=kt == KT - 1)
                last.then_inc(slot_full, 1)
            b = take()
            for t in range(NT):
                c, rc = divmod(t, RC)
                for kt in range(KT):
                    rows = xt[:, kt, rc * P * C:(rc + 1) * P * C].rearrange("x (p c) -> x c p", c=C)[:, c, :]
                    last = nc.tensor.matmul(b[:, 2 * t:2 * t + 2], rows, gate_x[:, kt, :], start=kt == 0, stop=kt == KT - 1)
            last.then_inc(slot_full, 1)
            pe.wait_ge(slot_free, SLOTS)

            with pe.Fori(0, C // 2) as it:
                def transposes(s):
                    par, jp = divmod(s, JP)
                    if jp == 0:
                        pe.wait_ge(adj_in[par], it * 16 + 16)
                    if s >= 4:
                        pe.wait_ge(t_free, it * STEPS + s - 3)
                    for jj in range(2):
                        for rc in range(RC):
                            j = 2 * jp + jj
                            last = nc.tensor.transpose(bank[4 + s % 4][:, (jj * RC + rc) * P:(jj * RC + rc + 1) * P],
                                                       adj_n[par][:, rc, j * P:(j + 1) * P], ident[:])
                    last.then_inc(t_full, 1)

                def products(s, acc, t_hi, t_lo, m_hi, m_lo, done):
                    jp = s % JP
                    for jj in range(2):
                        j = 2 * jp + jj
                        for rc in range(RC):
                            o, rows = bank[acc + rc][:, 0:GW], slice(rc * P, (rc + 1) * P)
                            first, end = jp == 0 and jj == 0, jp == JP - 1 and jj == 1
                            nc.tensor.matmul(o, t_hi[s % RING][:, jj, rows], m_hi[:, j, :], start=first, stop=False)
                            nc.tensor.matmul(o, t_hi[s % RING][:, jj, rows], m_lo[:, j, :], start=False, stop=False)
                            last = nc.tensor.matmul(o, t_lo[s % RING][:, jj, rows], m_hi[:, j, :], start=False, stop=end)
                    last.then_inc(done, 1)

                transposes(0)
                transposes(1)
                for s in range(STEPS + 1):
                    if s + 2 < STEPS:
                        transposes(s + 2)
                    if s < STEPS:
                        pe.wait_ge(t_free, it * STEPS + s + 1)
                        if s == 0:
                            pe.wait_ge(pg_copied, it * 2 + 1)
                        elif s == JP:
                            pe.wait_ge(pg_copied, it * 2 + 2)
                        products(s, 0, at_hi, at_lo, g_hi, g_lo, g_done)
                    if s >= 1:
                        pe.wait_ge(et_lo_ready, it * STEPS + s)
                        if s - 1 == 0:
                            pe.wait_ge(ph_copied, it * 2 + 1)
                        elif s - 1 == JP:
                            pe.wait_ge(ph_copied, it * 2 + 2)
                        products(s - 1, 2, et_hi, et_lo, h_hi, h_lo, h_done)

            pe.wait_ge(x1_ready, NT)
            n = 0
            for kt in range(KT):
                for rc in range(RC):
                    for ch in range(2):
                        for i in range(4):
                            last = nc.tensor.transpose(bank[n][:, i * P:(i + 1) * P], xn[:, rc, 4 * ch + i, kt * P:(kt + 1) * P], ident[:])
                        last.then_inc(x1t_full, 1)
                        n += 1

        @block.scalar
        def _(act):
            for s in range(PROJ0, LEFT0):
                j, which = divmod(s - PROJ0, 2)
                act.wait_ge(slot_full, s + 1)
                if which == 0:
                    nc.scalar.copy(g_hi[:, j, :], slot_bank[s][:, 0:GW]).then_inc(slot_hi, 1)
                else:
                    nc.scalar.copy(h_hi[:, j, 0:D], slot_bank[s][:, 0:D]).then_inc(slot_hi, 1)

            act.sem_inc(pg_copied)
            act.sem_inc(ph_copied)
            with act.Fori(0, C // 2) as it:
                def edge_weights(s):
                    act.wait_ge(leaky_ready, it * STEPS + s + 1)
                    nc.scalar.activation(e32[s % 2][:], leaky[s % 2][:], ACT.Exp, scale=-1.0).then_inc(e_ready, 1)
                    act.wait_ge(e_ready, it * STEPS + s + 1)
                    if s >= RING:
                        act.wait_ge(h_done, it * STEPS + s - RING + 1)
                    nc.scalar.copy(et_hi[s % RING][:], e32[s % 2][:]).then_inc(et_hi_ready, 1)

                def block_end(c, first):
                    if first:
                        act.wait_ge(g_done, it * STEPS + (c + 1) * JP)
                        act.wait_ge(mixed, it * 2 * LINKS + c * LINKS + 1)
                        nc.scalar.copy(pg[:, 0, :], bank[0][:, 0:GW])
                        nc.scalar.copy(pg[:, 1, :], bank[1][:, 0:GW]).then_inc(pg_copied, 1)
                    else:
                        act.wait_ge(h_done, it * STEPS + (c + 1) * JP)
                        nc.scalar.copy(ph[:, 0, :], bank[2][:, 0:GW])
                        nc.scalar.copy(ph[:, 1, :], bank[3][:, 0:GW]).then_inc(ph_copied, 1)

                def epilogue(c):
                    act.wait_ge(mixed, it * 2 * LINKS + c * LINKS + 2)
                    nc.scalar.activation(gates[:, 1], gates[:, 0], ACT.Exp, scale=-1.0).then_inc(gate_exp, 1)
                    act.wait_ge(mixed, it * 2 * LINKS + c * LINKS + 10)
                    nc.scalar.activation(mix[:, 1], mix[:, 0], ACT.Exp, scale=-1.0).then_inc(mix_exp, 1)

                for s in range(STEPS):
                    act.wait_ge(t_full, it * STEPS + s + 1)
                    if s >= RING:
                        act.wait_ge(g_done, it * STEPS + s - RING + 1)
                    nc.scalar.copy(at_hi[s % RING][:], bank[4 + s % 4][:].rearrange("p (j i) -> p j i", j=2)).then_inc(at_hi_ready, 1)
                    if s >= 1:
                        edge_weights(s - 1)
                    if s == JP:
                        block_end(0, True)
                    if s == JP + 1:
                        block_end(0, False)
                    if s == JP + 3:
                        epilogue(0)
                edge_weights(STEPS - 1)
                block_end(1, True)
                block_end(1, False)
                epilogue(1)

            act.wait_ge(rstd_step, 1)
            nc.scalar.activation(rstd[:, 1, :], rstd[:, 0, :], ACT.Sqrt).then_inc(std_ready, 1)
            for n in range(0, 8, 2):
                act.wait_ge(x1t_full, n + 1)
                kt, rc, ch = n // 4, n // 2 % 2, n % 2
                nc.scalar.copy(xt_dst(xt, kt, rc, ch), bank[n][:].rearrange("x (c p) -> x c p", c=4)).then_inc(x1t_ready, 1)

        @block.vector
        def _(dve):
            nc.vector.memset(ones[:], 1.0)
            nc.vector.memset(h_lo[:].bitcast(f32), 0.0)
            nc.vector.memset(h_hi[:, :, D + 1:GW].bitcast(f32), 0.0)
            nc.vector.memset(h_hi[:, :, D:D + 1].bitcast(f32), 1.0)
            dve.wait_ge(in_w, 32)
            dve.wait_ge(in_small, 128)
            for kt in range(KT):
                for o, dst in ((0, wl[:, kt, :]), (D, proj[:, kt, GW + D:GW + D + 1])):
                    nc.vector.tensor_tensor_reduce(out=junk[:], in0=proj[:, kt, GW:GW + D], in1=a_bc[:, o:o + D], scale=1.0,
                                                   scalar=0.0, op0=ALU.mult, op1=ALU.add, accum_out=dst).then_inc(wl_ready, 1)
                    dve.wait_ge(wl_ready, 2 * kt + (o > 0) + 1)
            for kt in range(KT):
                nc.vector.tensor_scalar(wl_rep[:, kt, :], ones[:], wl[:, kt, :], None, ALU.mult).then_inc(wl_done, 1)
            s = 0
            for kt in range(KT):
                for rc in range(RC):
                    for ch in range(2):
                        dve.wait_ge(slot_full, s + 1)
                        nc.vector.tensor_copy(xt_dst(xt, kt, rc, ch), slot_bank[s][:].rearrange("x (c p) -> x c p", c=4)).then_inc(slot_free, 1)
                        s += 1
            for s in range(PROJ0, LEFT0):
                j, which = divmod(s - PROJ0, 2)
                dve.wait_ge(slot_hi, s - PROJ0 + 1)
                if which == 0:
                    nc.vector.tensor_tensor(g_lo[:, j, :], slot_bank[s][:, 0:GW], g_hi[:, j, :].bitcast(f32), ALU.subtract).then_inc(slot_free, 1)
                else:
                    nc.vector.tensor_copy(s_right[:, j:j + 1], slot_bank[s][:, D:D + 1])
                    nc.vector.tensor_tensor(h_lo[:, j, 0:D], slot_bank[s][:, 0:D], h_hi[:, j, 0:D].bitcast(f32), ALU.subtract).then_inc(slot_free, 1)
            for q in range(QCH):
                s = LEFT0 + q
                dve.wait_ge(slot_full, s + 1)
                rc, half = divmod(q, 2)
                nc.vector.tensor_copy(s_left[:, :, rc, half * 64:half * 64 + 64],
                                      slot_bank[s][:].rearrange("x (p c) -> x c p", c=C)).then_inc(slot_free, 1)
            dve.wait_ge(slot_full, SLOTS)
            nc.vector.tensor_tensor(gate_xi[:, :, :], slot_bank[SLOTS - 1][:, 0:2 * NT].rearrange("p (t o) -> p t o", o=2),
                                    gate_b[:].rearrange("p (u o) -> p u o", u=1).broadcast_to((P, NT, 2)), ALU.add).then_inc(slot_free, 1)
            dve.wait_ge(slot_free, SLOTS)

            dve.sem_inc(mixed)
            with dve.Fori(0, C // 2) as it:
                def step(s):
                    par, jp = divmod(s, JP)
                    src, r, b = bank[4 + s % 4], s % RING, it * STEPS + s
                    tr = src[:].rearrange("p (j i) -> p j i", j=2)
                    dve.wait_ge(at_hi_ready, b + 1)
                    nc.vector.tensor_tensor(at_lo[r][:], tr, at_hi[r][:].bitcast(f32), ALU.subtract)
                    if s >= 1:
                        dve.wait_ge(z_ready, b)
                    nc.vector.tensor_scalar(off[:], tr, 0.0, BIG, ALU.is_equal, ALU.mult).then_inc(t_free, 1)
                    dve.wait_ge(t_free, b + 1)
                    if s >= 1:
                        dve.wait_ge(leaky_ready, b)
                    for jj in range(2):
                        j = 2 * jp + jj
                        row = s_left[:, bass.ds(it * 2 + par, 1)].rearrange("x o r p -> x (o r p)")
                        last = nc.vector.scalar_tensor_tensor(out=z[:, jj, :], in0=row, scalar=s_right[:, j:j + 1],
                                                              in1=off[:, jj, :], op0=ALU.add, op1=ALU.add)
                    last.then_inc(z_ready, 1)
                    dve.wait_ge(z_ready, b + 1)
                    if s >= 2:
                        dve.wait_ge(et_lo_ready, b - 1)
                    nc.vector.scalar_tensor_tensor(out=leaky[s % 2][:], in0=z[:], scalar=0.01, in1=z[:],
                                                   op0=ALU.mult, op1=ALU.max).then_inc(leaky_ready, 1)

                def edge_lo(s):
                    dve.wait_ge(et_hi_ready, it * STEPS + s + 1)
                    nc.vector.tensor_tensor(et_lo[s % RING][:], e32[s % 2][:], et_hi[s % RING][:].bitcast(f32),
                                            ALU.subtract).then_inc(et_lo_ready, 1)

                def count(par):
                    dve.wait_ge(adj_in[par], it * 16 + 16)
                    for rc in range(RC):
                        last = nc.vector.tensor_scalar(count_junk[:], adj_n[par][:, rc, :], 0.0, None, ALU.is_equal, ALU.add,
                                                       accum_out=masked_count[:, bass.ds(it * 4 + par * 2 + rc, 1)])
                        last.then_inc(counted if rc else masked_dve, 1)
                        if rc == 0:
                            dve.wait_ge(masked_dve, it * 2 + par + 1)
                    dve.wait_ge(counted, it * 2 + par + 1)

                def epilogue(c):
                    base, made = it * 2 * LINKS + c * LINKS, 0

                    def link(ins, wait=True):
                        nonlocal made
                        made += 1
                        ins.then_inc(mixed, 1)
                        if wait:
                            dve.wait_ge(mixed, base + made + 1)

                    t0 = it * 4 + c * 2
                    dve.wait_ge(pg_copied, it * 2 + c + 2)
                    dve.wait_ge(ph_copied, it * 2 + c + 2)
                    link(nc.vector.tensor_tensor(gates[:, 0], pg[:, :, D:D + 2], gate_xi[:, bass.ds(t0, 2), :], ALU.add))
                    link(nc.vector.tensor_tensor(mix[:, 0], pg[:, :, 0:D], b_bc[:].rearrange("p (u d) -> p u d", u=1).broadcast_to((P, RC, D)), ALU.add))
                    link(nc.vector.tensor_scalar(den[:, 0, :].rearrange("p (r o) -> p r o", o=1), ph[:, :, D:D + 1], 1e-5, None, ALU.add))
                    link(nc.vector.reciprocal(den[:, 1, :], den[:, 0, :]))
                    dve.wait_ge(gate_exp, it * 2 + c + 1)
                    link(nc.vector.tensor_scalar(gates[:, 2], gates[:, 1], 1.0, None, ALU.add))
                    link(nc.vector.reciprocal(gates[:, 0], gates[:, 2]))
                    link(nc.vector.tensor_tensor(gates[:, 2, :, 0:1], gates[:, 0, :, 0:1], den[:, 1, :].rearrange("p (r o) -> p r o", o=1), ALU.mult))
                    for rc in range(RC):
                        last = nc.vector.tensor_scalar(ph[:, rc, 0:D], ph[:, rc, 0:D], gates[:, 2, rc, 0:1], None, ALU.mult)
                    link(last)
                    for rc in range(RC):
                        last = nc.vector.scalar_tensor_tensor(out=mix[:, 0, rc, :], in0=mix[:, 0, rc, :], scalar=gates[:, 0, rc, 1:2],
                                                              in1=ph[:, rc, 0:D], op0=ALU.mult, op1=ALU.add)
                    link(last)
                    dve.wait_ge(mix_exp, it * 2 + c + 1)
                    link(nc.vector.tensor_scalar(mix[:, 1], mix[:, 1], 1.0, None, ALU.add))
                    link(nc.vector.reciprocal(mix[:, 0], mix[:, 1]))
                    xc = xn[:, :, bass.ds(it * 2 + c, 1), :].rearrange("p r o d -> p r (o d)")
                    link(nc.vector.tensor_tensor(xc, mix[:, 0], xc, ALU.add))
                    dve.sem_inc(dve_tick)
                    for rc in range(RC):
                        row = xn[:, rc, bass.ds(it * 2 + c, 1), :].rearrange("p o d -> p (o d)")
                        last = nc.vector.bn_stats(stats[:, rc, :], row)
                    link(last)
                    dve.sem_inc(dve_tick)
                    for rc in range(RC):
                        last = nc.vector.bn_aggr(moments[:, rc, :], stats[:, rc, :])
                    link(last)
                    link(nc.vector.tensor_copy(mv[:, bass.ds(t0, 2), :], moments[:]))
                    link(nc.vector.tensor_copy(junk[:, 0:1], ones[:, 0:1]))
                    assert made == LINKS

                for s in range(STEPS):
                    step(s)
                    if s >= 1:
                        edge_lo(s - 1)
                    if s in (1, JP + 1):
                        count(s // JP)
                    if s == JP + 3:
                        epilogue(0)
                edge_lo(STEPS - 1)
                epilogue(1)

            nc.vector.tensor_scalar(rstd[:, 0, :].rearrange("p (t o) -> p t o", o=1), mv[:, :, 1:2], g["LN_EPS"], None, ALU.add).then_inc(rstd_step, 1)
            dve.wait_ge(std_ready, 1)
            nc.vector.reciprocal(rstd[:, 2, :], rstd[:, 1, :]).then_inc(rstd_step, 1)
            dve.wait_ge(rstd_step, 2)
            for t in range(NT):
                c, rc = divmod(t, RC)
                nc.vector.tensor_scalar(xn[:, rc, c, :], xn[:, rc, c, :], mv[:, t, 0:1], rstd[:, 2, t:t + 1], ALU.subtract,
                                        ALU.mult).then_inc(x1_ready, 1)
            for n in range(1, 8, 2):
                dve.wait_ge(x1t_full, n + 1)
                kt, rc, ch = n // 4, n // 2 % 2, n % 2
                nc.vector.tensor_copy(xt_dst(xt, kt, rc, ch), bank[n][:].rearrange("x (c p) -> x c p", c=4)).then_inc(x1t_ready, 1)


def layer1(nc, g):
    f32, f32r, ALU, ACT, AX = g["f32"], g["f32r"], g["ALU"], g["ACT"], g["AX"]
    N, D, HEADS, C, R, RC, KT, NT = (g[k] for k in ("N", "D", "HEADS", "C", "R", "RC", "KT", "NT"))
    bank, ident, masked_count = g["bank"], g["ident"], g["masked_count"]
    NB = N // BANK
    TPB = BANK // P
    QCH = N // BANK
    CH = D * C // BANK
    PROBS = TPB + 1
    RING = 3
    HALF_SCALE = D ** -0.5 / 2

    PROJ = 2 * CH
    SLOTS_H = 3 * PROJ + NT * QCH + NB * TPB // 2
    SPLITS_H = 3 * CH

    ctx = ExitStack()
    with ctx:
        def sb(name, shape, dt=f32):
            return ctx.enter_context(nc.sbuf_tensor("l1_" + name, shape, dt))

        def sem(name):
            return ctx.enter_context(nc.semaphore("l1_" + name))

        kt_hi, kt_lo = sb("kt_hi", [P, KT, N], f32r), sb("kt_lo", [P, KT, N], f32r)
        v_hi, v_lo = sb("v_hi", [P, NT, D], f32r), sb("v_lo", [P, NT, D], f32r)
        qt_hi, qt_lo = sb("qt_hi", [P, KT, BANK], f32r), sb("qt_lo", [P, KT, BANK], f32r)
        probs = sb("probs", [P, PROBS, N])
        pt_hi, pt_lo = ([sb(f"pt_{w}{i}", [P, BANK], f32r) for i in range(RING)] for w in ("hi", "lo"))
        ot_hi, ot_lo = sb("ot_hi", [P, KT, BANK], f32r), sb("ot_lo", [P, KT, BANK], f32r)
        w_raw = [sb(f"w_raw{i}", [P, KT, BANK]) for i in range(2)]
        w_hi, w_lo = ([sb(f"w_{w}{i}", [P, KT, BANK], f32r) for i in range(2)] for w in ("hi", "lo"))
        xh_raw, xh_hi, xh_lo = sb("xh_raw", [P, KT, R]), sb("xh_hi", [P, KT, R], f32r), sb("xh_lo", [P, KT, R], f32r)
        wo_raw, wo_hi, wo_lo = sb("wo_raw", [P, KT, D]), sb("wo_hi", [P, KT, D], f32r), sb("wo_lo", [P, KT, D], f32r)
        bias_t = [sb(f"bias_t{i}", [P, N]) for i in range(2)]
        y = sb("y", [P, NT, D])
        maxes = sb("maxes", [P, NT, QCH + 1])
        row_max = sb("row_max", [P, NT, 1])
        exp_bias = sb("exp_bias", [P, NT])
        den = sb("den", [P, NT])
        capped, masked_exp, masked_sum, rden = (sb(n, [P, NT]) for n in ("capped", "masked_exp", "masked_sum", "rden"))
        ref_mask = sb("ref_mask", [P, 1])
        stats = sb("stats", [P, NT, 6])
        mv = sb("mv", [P, NT, 2])
        rstd = sb("rstd", [P, 3, NT])

        pool_tick, dve_tick = sem("pool_tick"), sem("dve_tick")
        ready, w_in, x_in, wo_in = sem("ready"), [sem("w_in0"), sem("w_in1")], sem("xh_in"), sem("wo_in")
        bias_in = [sem("bias_in0"), sem("bias_in1")]
        w_hi_ready, w_split = sem("w_hi_ready"), sem("w_split")
        xh_hi_ready, xh_split, wo_hi_ready, wo_split = sem("xh_hi_ready"), sem("xh_split"), sem("wo_hi_ready"), sem("wo_split")
        slot_full, slot_hi, slot_free = sem("slot_full"), sem("slot_hi"), sem("slot_free")
        max_ready, scores_ready, probs_ready = sem("max_ready"), sem("scores_ready"), sem("probs_ready")
        pt_full, pt_hi_ready, pt_split, pt_used = sem("pt_full"), sem("pt_hi_ready"), sem("pt_split"), sem("pt_used")
        ot_full, ot_hi_ready, ot_split = sem("ot_full"), sem("ot_hi_ready"), sem("ot_split")
        capped_ready, masked_ready, den_step = sem("capped_ready"), sem("masked_ready"), sem("den_step")
        floor_step, summed = sem("floor_step"), sem("summed")
        x1_in, y_step, std_ready, normed, out_done = sem("x1_in"), sem("y_step"), sem("std_ready"), sem("normed"), sem("out_done")

        class Walk:
            PER_HEAD = dict(slot=SLOTS_H, proj=3 * PROJ, split=SPLITS_H, head=1, tile=NT, block=NB, pt=NB * NT)

            def __init__(self):
                self.n = dict.fromkeys(self.PER_HEAD, 0)
                self.it = None
                self.out_slot = 0

            def at(self, what, k=0):
                here = self.n[what] + k
                return here if self.it is None else self.it * self.PER_HEAD[what] + here

            def past(self, what, k=1):
                self.n[what] += k

        def walk_heads(w, eng, start, rest, end):
            start()
            before = dict(w.n)
            with eng.Fori(0, HEADS - 1) as it:
                w.it = it
                rest()
            w.it = None
            for k, per in w.PER_HEAD.items():
                made = w.n[k] - before[k]
                assert made in (0, per), (k, made, per)
                w.n[k] += (HEADS - 2) * made
            w.out_slot += (HEADS - 2) * SLOTS_H
            end()

        def order(do, first):
            do.head_start()
            for j in range(CH):
                do.project("k", j)
            do.project("q", 0)
            if not first:
                do.attend(NB - 1)
                do.project_out(NB - 1)
            do.out_weights()
            for t in range(TPB):
                do.scores(0, t)
            do.project("q", 1)
            for j in range(CH):
                do.project("v", j)
            for nb in range(1, NB):
                do.scores(nb, 0)
                do.attend(nb - 1)
                for t in range(1, TPB):
                    do.scores(nb, t)
                if nb + 1 < NB:
                    do.project("q", nb + 1)
                do.project_out(nb - 1)

        def last_part(do):
            do.attend(NB - 1)
            do.project_out(NB - 1)

        WEIGHTS = ["k"] * CH + ["q"] * 2 + ["v"] * CH + ["q"] * 2
        CHUNK = list(range(CH)) + [0, 1] + list(range(CH)) + [2, 3]
        src_of = {"k": g["wk"], "q": g["wq"], "v": g["wv"]}

        block = ctx.enter_context(nc.Block())

        @block.gpsimd
        def _(pool):
            def load_w(i, h):
                v = src_of[WEIGHTS[i]].rearrange("(k p) n -> p k n", p=P)
                if h is None:
                    if i >= 2:
                        pool.wait_ge(w_split, i - 1)
                else:
                    pool.wait_ge(w_split, h * SPLITS_H + i - 1)
                    pool.sem_inc(pool_tick)
                pool.dma_start(w_raw[i % 2][:], v[:, :, CHUNK[i] * BANK:(CHUNK[i] + 1) * BANK]).then_inc(w_in[i % 2], 16)

            pool.dma_start(xh_raw[:], g["x1t_d"][:, :, 0:R]).then_inc(x_in, 16)
            load_w(0, None)
            load_w(1, None)
            pool.dma_start(wo_raw[:], g["wout"][0:D, :].rearrange("(k p) n -> p k n", p=P)).then_inc(wo_in, 16)
            for i in range(2, SPLITS_H):
                load_w(i, None)
            with pool.Fori(1, HEADS) as h:
                pool.wait_ge(xh_split, h)
                pool.sem_inc(pool_tick)
                pool.dma_start(xh_raw[:], g["x1t_d"][:, :, bass.ds(h * R, R)]).then_inc(x_in, 16)
                load_w(0, h)
                load_w(1, h)
                pool.wait_ge(wo_split, h)
                pool.sem_inc(pool_tick)
                pool.dma_start(wo_raw[:], g["wout"][bass.ds(h * D, D), :].rearrange("(k p) n -> p k n", p=P)).then_inc(wo_in, 16)
                for i in range(2, SPLITS_H):
                    load_w(i, h)

        @block.sync
        def _(sp):
            sp.dma_start(bias_t[0][:], g["bias_d"][0]).then_inc(bias_in[0], 16)
            sp.dma_start(bias_t[1][:], g["bias_d"][1]).then_inc(bias_in[1], 16)
            for t in range(2, NT):
                sp.wait_ge(max_ready, t - 1)
                sp.dma_start(bias_t[t % 2][:], g["bias_d"][t]).then_inc(bias_in[t % 2], 16)
            with sp.Fori(1, HEADS) as h:
                for t in range(NT):
                    sp.wait_ge(max_ready, h * NT + t - 1)
                    sp.dma_start(bias_t[t % 2][:], g["bias_d"][t]).then_inc(bias_in[t % 2], 16)
            sp.wait_ge(pt_full, HEADS * NB * NT)
            sp.dma_start(probs[:, 0:2, :].rearrange("p a n -> p (a n)"), g["x1_d"]).then_inc(x1_in, 16)
            out_v = g["out"].rearrange("(rc p c) d -> p c rc d", rc=RC, p=P)
            for c in range(C):
                sp.wait_ge(normed, RC * (c + 1))
                sp.dma_start(out_v[:, c], y[:, c * RC:(c + 1) * RC, :]).then_inc(out_done, 16)
            sp.wait_ge(out_done, 16 * C)

        @block.tensor
        def _(pe):
            w = Walk()

            def take():
                if w.it is not None or w.n["slot"] >= 4:
                    pe.wait_ge(slot_free, w.at("slot", -3))
                b = bank[w.n["slot"] % 4]
                w.past("slot")
                return b

            def three(o, a_hi, a_lo, b_hi, b_lo, start, stop):
                nc.tensor.matmul(o, a_hi, b_hi, start=start, stop=False)
                nc.tensor.matmul(o, a_hi, b_lo, start=False, stop=False)
                return nc.tensor.matmul(o, a_lo, b_hi, start=False, stop=stop)

            class Do:
                def head_start(self):
                    w.past("head")
                    pe.wait_ge(xh_split, w.at("head"))

                def out_weights(self):
                    pass

                def project(self, which, j):
                    wh, wl = w_hi[w.n["split"] % 2], w_lo[w.n["split"] % 2]
                    w.past("split")
                    pe.wait_ge(w_split, w.at("split"))
                    for i in range(2):
                        b = take()
                        if which == "v":
                            for k in range(KT):
                                rows = slice(i * P, (i + 1) * P)
                                last = three(b[:], xh_hi[:, k, rows], xh_lo[:, k, rows], wh[:, k, :], wl[:, k, :], k == 0, k == KT - 1)
                        else:
                            for ci in range(2):
                                for k in range(KT):
                                    cols = slice(ci * D + i * P, ci * D + (i + 1) * P)
                                    last = three(b[:, ci * R:(ci + 1) * R], wh[:, k, cols], wl[:, k, cols], xh_hi[:, k, :], xh_lo[:, k, :],
                                                 k == 0, k == KT - 1)
                        last.then_inc(slot_full, 1)

                def scores(self, nb, t):
                    if t == 0:
                        pe.wait_ge(slot_free, w.at("slot", -self.since_q))
                    for q in range(QCH):
                        b = take()
                        for k in range(KT):
                            rows, keys = slice(t * P, (t + 1) * P), slice(q * BANK, (q + 1) * BANK)
                            last = three(b[:], qt_hi[:, k, rows], qt_lo[:, k, rows], kt_hi[:, k, keys], kt_lo[:, k, keys], k == 0, k == KT - 1)
                        last.then_inc(slot_full, 1)

                def transposes(self, nb, k):
                    if w.it is not None or w.n["pt"] >= 2:
                        pe.wait_ge(pt_split, w.at("pt", -1))
                    for t in range(TPB):
                        last = nc.tensor.transpose(bank[4 + k % 2][:, t * P:(t + 1) * P],
                                                   probs[:, (nb * TPB + t) % PROBS, k * P:(k + 1) * P], ident[:])
                    last.then_inc(pt_full, 1)
                    w.past("pt")

                def attend(self, nb):
                    w.past("block")
                    pe.wait_ge(probs_ready, w.at("block") * TPB)
                    self.transposes(nb, 0)
                    self.transposes(nb, 1)
                    for k in range(NT):
                        if k + 2 < NT:
                            self.transposes(nb, k + 2)
                        behind = min(k + 3, NT)
                        pe.wait_ge(pt_split, w.at("pt", k + 1 - behind))
                        if k == 0 and (w.it is not None or w.n["block"] > 1):
                            pe.wait_ge(ot_split, w.at("block", -1))
                        ph, pl = pt_hi[(nb * NT + k) % RING], pt_lo[(nb * NT + k) % RING]
                        for d in range(KT):
                            cols = slice(d * P, (d + 1) * P)
                            last = three(bank[6 + d][:], v_hi[:, k, cols], v_lo[:, k, cols], ph[:], pl[:], k == 0, k == NT - 1)
                        last.then_inc(pt_used, 1)

                def project_out(self, nb):
                    pe.wait_ge(ot_split, w.at("block"))
                    pe.wait_ge(wo_split, w.at("head", self.wo_lag))
                    for pair in range(TPB // 2):
                        b = take()
                        for i in range(2):
                            t = 2 * pair + i
                            for k in range(KT):
                                rows = slice(t * P, (t + 1) * P)
                                last = three(b[:, i * D:(i + 1) * D], ot_hi[:, k, rows], ot_lo[:, k, rows], wo_hi[:, k, :], wo_lo[:, k, :],
                                             k == 0, k == KT - 1)
                        last.then_inc(slot_full, 1)

                since_q = 0
                wo_lag = 0

            do = Do()
            plain = (do.scores, do.project, do.project_out, do.out_weights, do.head_start)

            def scores(nb, t):
                if t == 0:
                    do.since_q = w.n["slot"] - do.q_slot
                plain[0](nb, t)

            def project(which, j):
                plain[1](which, j)
                if which == "q":
                    do.q_slot = w.n["slot"]

            def head_start():
                plain[4]()
                do.wo_lag = -1

            def out_weights():
                do.wo_lag = 0

            do.scores, do.project, do.head_start, do.out_weights = scores, project, head_start, out_weights

            walk_heads(w, pe, lambda: order(do, True), lambda: order(do, False), lambda: last_part(do))

        @block.scalar
        def _(act):
            w = Walk()

            class Do:
                def split(self, i):
                    act.wait_ge(w_in[i % 2], self.loads(i))
                    if self.guard is not None:
                        act.wait_ge(slot_full, self.guard)
                    nc.scalar.copy(w_hi[i % 2][:], w_raw[i % 2][:]).then_inc(w_hi_ready, 1)

                def loads(self, i):
                    n = 16 * (w.n["head"] - 1) * SPLITS_H // 2 + 16 * (i // 2 + 1)
                    return n if w.it is None else w.it * (8 * SPLITS_H) + n

                guard = None

                def head_start(self):
                    w.past("head")
                    act.wait_ge(x_in, 16 * w.at("head"))
                    if w.it is not None:
                        act.wait_ge(slot_full, w.at("slot"))
                    nc.scalar.copy(xh_hi[:], xh_raw[:]).then_inc(xh_hi_ready, 1)
                    self.i = 0
                    self.guard = w.at("slot") if w.it is not None else None
                    self.split(0)

                def out_weights(self):
                    act.wait_ge(wo_in, 16 * w.at("head"))
                    if w.it is not None:
                        act.wait_ge(slot_full, w.at("slot"))
                    nc.scalar.copy(wo_hi[:], wo_raw[:]).then_inc(wo_hi_ready, 1)

                def project(self, which, j):
                    self.i += 1
                    if self.i < SPLITS_H:
                        self.guard = w.at("slot") if (w.it is not None or w.n["slot"]) else None
                        self.split(self.i)
                    for i in range(2):
                        b = bank[w.n["slot"] % 4]
                        w.past("slot")
                        w.past("proj")
                        act.wait_ge(slot_full, w.at("slot"))
                        if which == "k":
                            nc.scalar.copy(kt_hi[:, i, j * BANK:(j + 1) * BANK], b[:]).then_inc(slot_hi, 1)
                        elif which == "q":
                            nc.scalar.mul(qt_hi[:, i, :], b[:], HALF_SCALE).then_inc(slot_hi, 1)
                        else:
                            dst = v_hi[:, 4 * j:4 * j + 4, :].rearrange("p (c r) d -> p r c d", r=RC)[:, i]
                            nc.scalar.copy(dst, b[:].rearrange("p (c d) -> p c d", c=2)).then_inc(slot_hi, 1)

                pending = None

                def scores(self, nb, t):
                    for q in range(QCH):
                        w.past("slot")
                    w.past("tile")
                    if t == 0 and nb > 0:
                        self.pending = (nb, t, w.at("tile"))
                    else:
                        self.exponentials(nb, t, w.at("tile"))

                def exponentials(self, nb, t, tile):
                    n = nb * TPB + t
                    p = probs[:, n % PROBS, :]
                    act.wait_ge(scores_ready, tile)
                    nc.scalar.activation(p, p, ACT.Exp, bias=exp_bias[:, n:n + 1], scale=2.0, accum_out=den[:, n:n + 1]).then_inc(probs_ready, 1)

                def attend(self, nb):
                    w.past("block")
                    for k in range(NT):
                        w.past("pt")
                        act.wait_ge(pt_full, w.at("pt"))
                        if w.it is not None or w.n["pt"] > RING:
                            act.wait_ge(pt_used, w.at("pt", -RING))
                        nc.scalar.copy(pt_hi[(nb * NT + k) % RING][:], bank[4 + k % 2][:]).then_inc(pt_hi_ready, 1)
                        if k == 1 and self.pending:
                            self.exponentials(*self.pending)
                            self.pending = None
                    act.wait_ge(pt_used, w.at("pt"))
                    if w.it is not None or w.n["block"] > 1:
                        act.wait_ge(slot_full, w.at("slot", w.out_slot - w.n["slot"]))
                    for d in range(KT):
                        nc.scalar.copy(ot_hi[:, d, :], bank[6 + d][:]).then_inc(ot_hi_ready, 1)
                    cols = slice(nb * TPB, (nb + 1) * TPB)
                    act.wait_ge(capped_ready, w.at("block"))
                    nc.scalar.activation(masked_exp[:, cols], capped[:, cols], ACT.Exp, bias=ref_mask[:, 0:1]).then_inc(masked_ready, 1)

                def project_out(self, nb):
                    w.past("slot", TPB // 2)
                    w.out_slot = w.n["slot"]

            do = Do()

            act.wait_ge(ready, 1)
            walk_heads(w, act, lambda: order(do, True), lambda: order(do, False), lambda: last_part(do))
            act.wait_ge(y_step, 2)
            nc.scalar.activation(rstd[:, 1, :], rstd[:, 0, :], ACT.Sqrt).then_inc(std_ready, 1)

        @block.vector
        def _(dve):
            w = Walk()

            class Do:
                def lo(self, dst, src, hi):
                    return nc.vector.tensor_tensor(dst, src, hi.bitcast(f32), ALU.subtract)

                def split(self, i):
                    w.past("split")
                    dve.wait_ge(w_hi_ready, w.at("split"))
                    self.lo(w_lo[i % 2][:], w_raw[i % 2][:], w_hi[i % 2][:]).then_inc(w_split, 1)

                def head_start(self):
                    w.past("head")
                    dve.wait_ge(xh_hi_ready, w.at("head"))
                    self.lo(xh_lo[:], xh_raw[:], xh_hi[:]).then_inc(xh_split, 1)
                    self.i = 0
                    self.split(0)

                def out_weights(self):
                    dve.wait_ge(wo_hi_ready, w.at("head"))
                    self.lo(wo_lo[:], wo_raw[:], wo_hi[:]).then_inc(wo_split, 1)

                def project(self, which, j):
                    self.i += 1
                    if self.i < SPLITS_H:
                        self.split(self.i)
                    for i in range(2):
                        b = bank[w.n["slot"] % 4]
                        w.past("slot")
                        w.past("proj")
                        dve.wait_ge(slot_hi, w.at("proj"))
                        if which == "k":
                            keys = slice(j * BANK, (j + 1) * BANK)
                            last = self.lo(kt_lo[:, i, keys], b[:], kt_hi[:, i, keys])
                        elif which == "q":
                            last = nc.vector.scalar_tensor_tensor(out=qt_lo[:, i, :], in0=b[:], scalar=HALF_SCALE, in1=qt_hi[:, i, :].bitcast(f32),
                                                                  op0=ALU.mult, op1=ALU.subtract)
                        else:
                            def part(t):
                                return t[:, 4 * j:4 * j + 4, :].rearrange("p (c r) d -> p r c d", r=RC)[:, i]
                            last = self.lo(part(v_lo), b[:].rearrange("p (c d) -> p c d", c=2), part(v_hi))
                        last.then_inc(slot_free, 1)

                def scores(self, nb, t):
                    n = nb * TPB + t
                    w.past("tile")
                    dve.wait_ge(bias_in[n % 2], self.bias_loads(n))
                    if n >= PROBS:
                        dve.wait_ge(pt_full, w.at("pt"))
                    for q in range(QCH):
                        b = bank[w.n["slot"] % 4]
                        w.past("slot")
                        keys = slice(q * BANK, (q + 1) * BANK)
                        dve.wait_ge(slot_full, w.at("slot"))
                        dve.sem_inc(dve_tick)
                        nc.vector.tensor_tensor_reduce(out=probs[:, n % PROBS, keys], in0=b[:], in1=bias_t[n % 2][:, keys], scale=1.0, scalar=LOWEST,
                                                       op0=ALU.add, op1=ALU.max, accum_out=maxes[:, n, q:q + 1]).then_inc(slot_free, 1)
                    dve.wait_ge(slot_free, w.at("slot"))
                    nc.vector.tensor_reduce(out=row_max[:, n, :], in_=maxes[:, n, :], axis=AX.X, op=ALU.max).then_inc(max_ready, 1)
                    dve.wait_ge(max_ready, w.at("tile"))
                    nc.vector.tensor_scalar(exp_bias[:, n:n + 1], row_max[:, n, :], -2.0, None, ALU.mult).then_inc(scores_ready, 1)
                    if t == TPB - 1:
                        cols = slice(nb * TPB, (nb + 1) * TPB)
                        dve.wait_ge(scores_ready, w.at("tile"))
                        nc.vector.tensor_scalar(capped[:, cols], exp_bias[:, cols], -REF_MASK, None, ALU.min).then_inc(capped_ready, 1)

                def bias_loads(self, n):
                    k = 16 * ((w.n["tile"] - 1) // NT) * (NT // 2) + 16 * (n // 2 + 1)
                    return k if w.it is None else w.it * (8 * NT) + k

                def attend(self, nb):
                    w.past("block")
                    for k in range(NT):
                        w.past("pt")
                        r = (nb * NT + k) % RING
                        dve.wait_ge(pt_hi_ready, w.at("pt"))
                        self.lo(pt_lo[r][:], bank[4 + k % 2][:], pt_hi[r][:]).then_inc(pt_split, 1)
                    dve.wait_ge(ot_hi_ready, w.at("block") * KT)
                    for d in range(KT):
                        last = self.lo(ot_lo[:, d, :], bank[6 + d][:], ot_hi[:, d, :])
                    last.then_inc(ot_split, 1)
                    cols = slice(nb * TPB, (nb + 1) * TPB)
                    dve.wait_ge(masked_ready, w.at("block"))
                    nc.vector.tensor_tensor(masked_sum[:, cols], masked_exp[:, cols], masked_count[:, cols], ALU.mult).then_inc(den_step, 1)
                    dve.wait_ge(den_step, w.at("block") * 3 - 2)
                    nc.vector.tensor_tensor(masked_sum[:, cols], masked_sum[:, cols], den[:, cols], ALU.add).then_inc(den_step, 1)
                    dve.wait_ge(den_step, w.at("block") * 3 - 1)
                    nc.vector.reciprocal(rden[:, cols], masked_sum[:, cols]).then_inc(den_step, 1)

                def project_out(self, nb):
                    dve.wait_ge(den_step, w.at("block") * 3)
                    for pair in range(TPB // 2):
                        b = bank[w.n["slot"] % 4]
                        w.past("slot")
                        dve.wait_ge(slot_full, w.at("slot"))
                        for i in range(2):
                            n = nb * TPB + 2 * pair + i
                            last = nc.vector.scalar_tensor_tensor(out=y[:, n, :], in0=b[:, i * D:(i + 1) * D], scalar=rden[:, n:n + 1],
                                                                  in1=y[:, n, :], op0=ALU.mult, op1=ALU.add)
                        last.then_inc(slot_free, 1)

            do = Do()

            nc.vector.memset(y[:], 0.0)
            nc.vector.memset(ref_mask[:], REF_MASK).then_inc(y_step, 1)
            dve.wait_ge(y_step, 1)
            floor = maxes[:, :, QCH:QCH + 1]
            nc.vector.tensor_scalar(row_max[:], masked_count[:].rearrange("p (t o) -> p t o", o=1), 0.0, -LOWEST, ALU.is_equal, ALU.mult).then_inc(floor_step, 1)
            dve.wait_ge(floor_step, 1)
            nc.vector.tensor_scalar(floor, row_max[:], -1.0, REF_MASK / 2, ALU.mult, ALU.add).then_inc(ready, 1)
            dve.wait_ge(ready, 1)
            walk_heads(w, dve, lambda: order(do, True), lambda: order(do, False), lambda: last_part(do))

            dve.wait_ge(x1_in, 16)
            dve.wait_ge(slot_free, HEADS * SLOTS_H)
            x1 = probs[:, 0:2, :].rearrange("p a (c d) -> p a c d", d=D)
            for rc in range(RC):
                yc = y[:].rearrange("p (c r) d -> p r c d", r=RC)[:, rc]
                last = nc.vector.tensor_tensor(yc, yc, x1[:, rc], ALU.add)
            last.then_inc(summed, 1)
            dve.wait_ge(summed, 1)
            for t in range(NT):
                last = nc.vector.bn_stats(stats[:, t, :], y[:, t, :])
            last.then_inc(summed, 1)
            dve.wait_ge(summed, 2)
            for t in range(NT):
                last = nc.vector.bn_aggr(mv[:, t, :], stats[:, t, :])
            last.then_inc(summed, 1)
            dve.wait_ge(summed, 3)
            nc.vector.tensor_scalar(rstd[:, 0, :].rearrange("p (t o) -> p t o", o=1), mv[:, :, 1:2], g["LN_EPS"], None, ALU.add).then_inc(y_step, 1)
            dve.wait_ge(std_ready, 1)
            nc.vector.reciprocal(rstd[:, 2, :], rstd[:, 1, :]).then_inc(summed, 1)
            dve.wait_ge(summed, 4)
            for t in range(NT):
                nc.vector.tensor_scalar(y[:, t, :], y[:, t, :], mv[:, t, 0:1], rstd[:, 2, t:t + 1], ALU.subtract,
                                        ALU.mult).then_inc(normed, 1)


_INS = ["x", "adj", "L0_gnn_W_sa", "L0_gnn_a_sa", "L0_gnn_W_gcnb", "L0_gnn_b_gcnb", "L0_gnn_Wa", "L0_gnn_ba",
        "L0_gnn_Wb", "L0_gnn_bb", "L1_gnn_Wq", "L1_gnn_Wk", "L1_gnn_Wv", "L1_gnn_Wout"]


def kernel(**inputs):
    import numpy as _np
    import concourse.bacc as _bacc
    from concourse import mybir as _mybir
    from concourse.bass_utils import run_bass_kernel_spmd as _run

    nc = _bacc.Bacc("TRN2", target_bir_lowering=False, num_devices=1)
    arrays, args = {}, []
    for name in _INS:
        a = _np.ascontiguousarray(inputs[name])
        arrays[f"in_{name}_dram"] = a
        args.append(nc.dram_tensor(f"in_{name}_dram", a.shape, _mybir.dt.from_np(a.dtype), kind="ExternalInput").ap())
    args.append(nc.dram_tensor("out_0_dram", (2048, 256), _mybir.dt.float32, kind="ExternalOutput").ap())
    gnn_two_layers(nc, *args)
    r = _run(nc, [arrays], core_ids=[0])
    return r.results[0]["out_0_dram"]
```

```python
import concourse.bass as bass
from concourse import mybir
from contextlib import ExitStack

P = 128
BANK = 512
BIG = float(2 ** 100)
REF_MASK = -1.0e6
LOWEST = -3.0e38


def gnn_two_layers(nc, x, adj, w_sa, a_sa, w_gcnb, b_gcnb, wa, ba, wb, bb, wq, wk, wv, wout, out):
    f32, f32r = mybir.dt.float32, mybir.dt.float32r
    ALU, ACT, AX = mybir.AluOpType, mybir.ActivationFunctionType, mybir.AxisListType

    N, D = x.shape
    HEADS = wq.shape[1] // D
    C = HEADS
    R = N // C
    KT = D // P
    RC = R // P
    NT = N // P
    QCH = N // BANK
    LN_EPS = 1e-5

    bias_d = nc.dram_tensor("bias_scratch", (NT, P, N), f32, kind="Internal").ap()
    x1_d = nc.dram_tensor("x1_scratch", (P, NT * D), f32, kind="Internal").ap()
    x1t_d = nc.dram_tensor("x1t_scratch", (P, KT, N), f32, kind="Internal").ap()

    whole = ExitStack()
    with whole:
        bank = [whole.enter_context(nc.psum_tensor(f"bank{i}", [P, BANK], f32)) for i in range(8)]

        def keep(name, shape, dt=f32):
            return whole.enter_context(nc.sbuf_tensor(name, shape, dt))

        ident = keep("ident", [P, P])
        masked_count = keep("masked_count", [P, NT])
        layer0(nc, locals())
        layer1(nc, locals())




def layer0(nc, g):
    f32, f32r, ALU, ACT = g["f32"], g["f32r"], g["ALU"], g["ACT"]
    N, D, C, RC, KT, NT, QCH = (g[k] for k in ("N", "D", "C", "RC", "KT", "NT", "QCH"))
    bank, ident, masked_count = g["bank"], g["ident"], g["masked_count"]
    GW = D + 2
    HW = D + 1
    RING = 4
    JP = NT // 2
    TURN = 2 * JP
    IB = RC * P
    ADDS = 4
    LINKS = 14

    ctx = ExitStack()
    with ctx:
        def sb(name, shape, dt=f32):
            return ctx.enter_context(nc.sbuf_tensor("l0_" + name, shape, dt))

        def sem(name):
            return ctx.enter_context(nc.semaphore("l0_" + name))

        xn = sb("xn", [P, RC, C, D])
        xt = sb("xt", [P, KT, N])
        gate_x = sb("gate_x", [P, KT, 2])
        wl = sb("wl", [P, KT, 1])
        ones = sb("ones", [P, P])
        b_bc = sb("b_bc", [P, D])
        gate_b = sb("gate_b", [P, 2])
        junk = sb("junk", [P, D])
        g_hi, g_lo = sb("g_hi", [P, NT, GW], f32r), sb("g_lo", [P, NT, GW], f32r)
        h_hi, h_lo = sb("h_hi", [P, NT, GW], f32r), sb("h_lo", [P, NT, GW], f32r)
        s_right = sb("s_right", [P, NT])
        s_left = sb("s_left", [P, C, RC, P])
        gate_xi = sb("gate_xi", [P, NT, 2])
        adj_n = [sb(f"adj_n{i}", [P, RC, N]) for i in range(2)]
        at_hi, at_lo = ([sb(f"at_{w}{i}", [P, 2, IB], f32r) for i in range(RING)] for w in ("hi", "lo"))
        et_hi, et_lo = ([sb(f"et_{w}{i}", [P, 2, IB], f32r) for i in range(RING)] for w in ("hi", "lo"))
        off = sb("off", [P, 2, IB])
        z = sb("z", [P, 2, IB])
        edge = [sb(f"edge{i}", [P, 2, IB]) for i in range(2)]
        bias_t = [sb(f"bias_t{i}", [P, C, N // C]) for i in range(RC)]
        count_junk = sb("count_junk", [P, N], mybir.dt.uint8)
        pg, ph = sb("pg", [P, RC, GW]), sb("ph", [P, RC, GW])
        gates = sb("gates", [P, 3, RC, 2])
        den = sb("den", [P, 2, RC])
        mix = sb("mix", [P, 2, RC, D])
        stats = sb("stats", [P, RC, 6])
        moments = sb("moments", [P, RC, 2])
        rstd = sb("rstd", [P, 3, RC])

        early = bias_t[1][:].rearrange("p c r -> p (c r)")
        proj = early[:, 0:KT * (GW + HW)].rearrange("p (k n) -> p k n", k=KT)
        a_bc = early[:, KT * (GW + HW):KT * (GW + HW) + 2 * D]
        wl_rep = early[:, KT * (GW + HW) + 2 * D:KT * (GW + HW) + 2 * D + KT * P].rearrange("p (k n) -> p k n", k=KT)

        dve_tick, sp_tick = sem("dve_tick"), sem("sp_tick")
        ident_ready, in_x, in_w, in_small = sem("ident_ready"), [sem(f"in_x{i}") for i in range(4)], sem("in_w"), sem("in_small")
        wl_ready, wl_done = sem("wl_ready"), sem("wl_done")
        slot_full, slot_hi, slot_free = sem("slot_full"), sem("slot_hi"), sem("slot_free")
        adj_in = [sem(f"adj_in{i}") for i in range(2)]
        t_full, at_hi_ready, t_free = sem("t_full"), sem("at_hi_ready"), sem("t_free")
        z_ready, leaky_ready, e_ready, et_hi_ready, et_lo_ready = (
            sem("z_ready"), sem("leaky_ready"), sem("e_ready"), sem("et_hi_ready"), sem("et_lo_ready"))
        g_done, h_done = sem("g_done"), sem("h_done")
        pg_copied, ph_copied = sem("pg_copied"), sem("ph_copied")
        mask_ready, counted, bias_added = sem("mask_ready"), sem("counted"), sem("bias_added")
        bias_stored = [sem(f"bias_stored{i}") for i in range(RC)]
        mixed, gate_tanh, mix_tanh, std_ready = sem("mixed"), sem("gate_tanh"), sem("mix_tanh"), sem("std_ready")
        x1_ready, x1t_full, x1t_ready, stored = (sem("x1_ready"), sem("x1t_full"), sem("x1t_ready"), sem("stored"))

        adj_v = g["adj"].rearrange("(rc p c) m -> c p rc m", rc=RC, p=P)
        XT_SLOTS = KT * RC * 2
        PROJ0 = XT_SLOTS
        LEFT0 = PROJ0 + 2 * NT
        GATE0 = LEFT0 + QCH
        SLOTS = GATE0 + 1
        slot_bank = [bank[4 + i % 4] for i in range(SLOTS)]

        def xt_order():
            return [(kt, rc, ch) for rc in range(RC) for ch in range(2) for kt in range(KT)]

        def xt_dst(t, kt, rc, ch):
            v = t[:, kt, rc * P * C:(rc + 1) * P * C].rearrange("x (p c) -> x c p", c=C)
            return v[:, 4 * ch:4 * ch + 4, :]

        class Turn:
            def __init__(self, kind, it):
                self.kind, self.it = kind, it

            def live(self, back):
                return {"first": back >= 0, "loop": True, "drain": back < 0}[self.kind]

            def step(self, s, lag):
                return s - lag if self.live(s - lag) else None

            def block(self, s, at):
                b, m = divmod(s - at, JP)
                return b if m == 0 and self.live(b) else None

            def n(self, per_step, k):
                return self.it * (per_step * TURN) + k

            def blocks(self, per_block, k):
                return self.it * (per_block * 2) + k

        def turns(eng, body):
            body(Turn("first", 0), TURN)
            with eng.Fori(1, C // 2) as it:
                body(Turn("loop", it), TURN)
            body(Turn("drain", C // 2), JP + 3)

        def wait(eng, s, value):
            if not (isinstance(value, int) and value <= 0):
                eng.wait_ge(s, value)

        block = ctx.enter_context(nc.Block())

        @block.sync
        def _(sp):
            xv = g["x"].rearrange("(rc p c) d -> p rc c d", rc=RC, p=P)
            for i in (0, 2):
                rc, ch = divmod(i, 2)
                sp.dma_start(xn[:, rc, 4 * ch:4 * ch + 4, :], xv[:, rc, 4 * ch:4 * ch + 4, :]).then_inc(in_x[i], 16)
            sp.dma_start(proj[:, :, 0:D], g["w_gcnb"].rearrange("(k p) n -> p k n", p=P)).then_inc(in_w, 16)
            sp.dma_start(proj[:, :, GW:GW + D], g["w_sa"].rearrange("(k p) n -> p k n", p=P)).then_inc(in_w, 16)
            sp.dma_start(adj_n[0][:], adj_v[0]).then_inc(adj_in[0], 16)
            sp.dma_start(adj_n[1][:], adj_v[1]).then_inc(adj_in[1], 16)

            def store(c, tile, rc):
                sp.wait_ge(bias_added, c * (ADDS * RC) + ADDS * (rc + 1))
                sp.sem_inc(sp_tick)
                sp.dma_start(g["bias_d"][tile].rearrange("o p n -> (o p) n"),
                             bias_t[rc][:].rearrange("p c r -> p (c r)")).then_inc(bias_stored[rc], 16)

            with sp.Fori(0, C // 2 - 1) as it:
                for par in range(2):
                    for rc in range(RC):
                        store(it * 2 + par, bass.ds(it * 4 + par * RC + rc, 1), rc)
                    sp.wait_ge(t_full, it * TURN + (par + 1) * JP)
                    sp.sem_inc(sp_tick)
                    sp.dma_start(adj_n[par][:], adj_v[bass.ds(it * 2 + 2 + par, 1)].rearrange(
                        "o p rc m -> (o p) rc m")).then_inc(adj_in[par], 16)
            for c in (C - 2, C - 1):
                for rc in range(RC):
                    store(c, slice(c * RC + rc, c * RC + rc + 1), rc)
            sp.wait_ge(x1t_ready, XT_SLOTS)
            sp.dma_start(g["x1t_d"], xt[:]).then_inc(stored, 16)
            sp.wait_ge(x1_ready, C)
            sp.dma_start(g["x1_d"], xn[:].rearrange("p r c d -> p (r c d)")).then_inc(stored, 16)
            sp.wait_ge(stored, 32)
            for rc in range(RC):
                sp.wait_ge(bias_stored[rc], 16 * C)

        @block.gpsimd
        def _(pool):
            nc.gpsimd.memset(ident[:], 0.0).then_inc(ident_ready, 1)
            pool.wait_ge(ident_ready, 1)
            nc.gpsimd.affine_select(out=ident[:], in_=ident[:], compare_op=ALU.not_equal, fill=1.0, base=0,
                                    pattern=[[-1, P]], channel_multiplier=1).then_inc(ident_ready, 1)
            pool.dma_start(a_bc, g["a_sa"].partition_broadcast(P)).then_inc(in_small, 16)
            for i, w in enumerate((g["wa"], g["wb"])):
                col = w.rearrange("o (s k p) -> p s k o", s=2, p=P)
                pool.dma_start(proj[:, :, D + i:D + i + 1], col[:, 0], allow_slow_non_contiguous=True).then_inc(in_small, 16)
                pool.dma_start(gate_x[:, :, i:i + 1], col[:, 1], allow_slow_non_contiguous=True).then_inc(in_small, 16)
            pool.dma_start(b_bc[:], g["b_gcnb"].partition_broadcast(P)).then_inc(in_small, 16)
            for i, b in enumerate((g["ba"], g["bb"])):
                pool.dma_start(gate_b[:, i:i + 1], b.partition_broadcast(P)).then_inc(in_small, 16)

            def body(turn, steps):
                for s in range(steps):
                    if (e := turn.step(s, 1)) is not None:
                        wait(pool, et_hi_ready, turn.n(1, e + 1))
                        wait(pool, h_done, turn.n(1, e + 1 - RING))
                        nc.gpsimd.tensor_tensor(et_lo[e % RING][:], edge[e % 2][:], et_hi[e % RING][:].bitcast(f32),
                                                ALU.subtract).then_inc(et_lo_ready, 1)
                    part, rc = s % ADDS, s // ADDS % RC
                    rc = 1 - rc
                    if (c := turn.block(s, ADDS * (rc + 1) + part)) is not None:
                        wait(pool, counted, turn.blocks(RC, c * RC + rc + 1))
                        cols = slice(C // ADDS * part, C // ADDS * (part + 1))
                        src = adj_n[c % 2][:, rc, :].rearrange("p (r c) -> p c r", c=C)[:, cols, :]
                        nc.gpsimd.tensor_tensor(bias_t[rc][:, cols, :], bias_t[rc][:, cols, :], src, ALU.add).then_inc(bias_added, 1)

            turns(pool, body)

        @block.tensor
        def _(pe):
            pe.wait_ge(ident_ready, 2)
            slot = 0

            def take():
                nonlocal slot
                if slot >= 4:
                    pe.wait_ge(slot_free, slot - 3)
                slot += 1
                return slot_bank[slot - 1]

            for kt, rc, ch in xt_order():
                pe.wait_ge(in_x[2 * rc + ch], 16)
                b = take()
                for i in range(4):
                    last = nc.tensor.transpose(b[:, i * P:(i + 1) * P], xn[:, rc, 4 * ch + i, kt * P:(kt + 1) * P], ident[:])
                last.then_inc(slot_full, 1)
            pe.wait_ge(slot_free, XT_SLOTS)
            pe.wait_ge(in_w, 32)
            pe.wait_ge(in_small, 128)
            pe.wait_ge(wl_ready, 4)
            for j in range(NT):
                for o, w in ((0, GW), (GW, HW)):
                    b = take()
                    for kt in range(KT):
                        last = nc.tensor.matmul(b[:, 0:w], xt[:, kt, j * P:(j + 1) * P], proj[:, kt, o:o + w],
                                                start=kt == 0, stop=kt == KT - 1)
                    last.then_inc(slot_full, 1)
            pe.wait_ge(wl_done, KT)
            for q in range(QCH):
                b = take()
                for kt in range(KT):
                    last = nc.tensor.matmul(b[:], wl_rep[:, kt, :], xt[:, kt, q * BANK:(q + 1) * BANK],
                                            start=kt == 0, stop=kt == KT - 1)
                last.then_inc(slot_full, 1)
            b = take()
            for t in range(NT):
                c, rc = divmod(t, RC)
                for kt in range(KT):
                    rows = xt[:, kt, rc * P * C:(rc + 1) * P * C].rearrange("x (p c) -> x c p", c=C)[:, c, :]
                    last = nc.tensor.matmul(b[:, 2 * t:2 * t + 2], rows, gate_x[:, kt, :], start=kt == 0, stop=kt == KT - 1)
            last.then_inc(slot_full, 1)
            pe.wait_ge(slot_free, SLOTS)

            def products(s, acc, t_hi, t_lo, m_hi, m_lo, done):
                jp = s % JP
                for jj in range(2):
                    j = 2 * jp + jj
                    for rc in range(RC):
                        o, rows = bank[acc + rc][:, 0:GW], slice(rc * P, (rc + 1) * P)
                        first, end = jp == 0 and jj == 0, jp == JP - 1 and jj == 1
                        nc.tensor.matmul(o, t_hi[s % RING][:, jj, rows], m_hi[:, j, :], start=first, stop=False)
                        nc.tensor.matmul(o, t_hi[s % RING][:, jj, rows], m_lo[:, j, :], start=False, stop=False)
                        last = nc.tensor.matmul(o, t_lo[s % RING][:, jj, rows], m_hi[:, j, :], start=False, stop=end)
                last.then_inc(done, 1)

            def body(turn, steps):
                for s in range(steps):
                    if (t := turn.step(s, 0)) is not None:
                        par, jp = divmod(t, JP)
                        if jp == 0:
                            pe.wait_ge(adj_in[par], turn.it * 16 + 16)
                        wait(pe, t_free, turn.n(1, t - 3))
                        for jj in range(2):
                            for rc in range(RC):
                                j = 2 * jp + jj
                                last = nc.tensor.transpose(bank[4 + t % 4][:, (jj * RC + rc) * P:(jj * RC + rc + 1) * P],
                                                           adj_n[par][:, rc, j * P:(j + 1) * P], ident[:])
                        last.then_inc(t_full, 1)
                    if (t := turn.step(s, 2)) is not None:
                        wait(pe, t_free, turn.n(1, t + 1))
                        if t % JP == 0:
                            wait(pe, pg_copied, turn.blocks(1, t // JP))
                        products(t, 0, at_hi, at_lo, g_hi, g_lo, g_done)
                    if (t := turn.step(s, 4)) is not None:
                        wait(pe, et_lo_ready, turn.n(1, t + 1))
                        if t % JP == 0:
                            wait(pe, ph_copied, turn.blocks(1, t // JP))
                        products(t, 2, et_hi, et_lo, h_hi, h_lo, h_done)

            turns(pe, body)

            pe.wait_ge(x1_ready, C)
            for n, (kt, rc, ch) in enumerate(xt_order()):
                for i in range(4):
                    last = nc.tensor.transpose(bank[n][:, i * P:(i + 1) * P], xn[:, rc, 4 * ch + i, kt * P:(kt + 1) * P], ident[:])
                last.then_inc(x1t_full, 1)

        @block.scalar
        def _(act):
            xv = g["x"].rearrange("(rc p c) d -> p rc c d", rc=RC, p=P)
            for i in (1, 3):
                rc, ch = divmod(i, 2)
                act.dma_start(xn[:, rc, 4 * ch:4 * ch + 4, :], xv[:, rc, 4 * ch:4 * ch + 4, :]).then_inc(in_x[i], 16)
            for s in range(PROJ0, LEFT0):
                j, which = divmod(s - PROJ0, 2)
                act.wait_ge(slot_full, s + 1)
                if which == 0:
                    nc.scalar.copy(g_hi[:, j, :], slot_bank[s][:, 0:GW]).then_inc(slot_hi, 1)
                else:
                    nc.scalar.copy(h_hi[:, j, 0:D], slot_bank[s][:, 0:D]).then_inc(slot_hi, 1)

            def body(turn, steps):
                def mixed_at(c, k):
                    return turn.blocks(LINKS, c * LINKS + k)

                for s in range(steps):
                    if (t := turn.step(s, 0)) is not None:
                        act.wait_ge(t_full, turn.n(1, t + 1))
                        wait(act, g_done, turn.n(1, t + 1 - RING))
                        nc.scalar.copy(at_hi[t % RING][:], bank[4 + t % 4][:].rearrange("p (j i) -> p j i", j=2)).then_inc(at_hi_ready, 1)
                    if (e := turn.step(s, 1)) is not None:
                        act.wait_ge(leaky_ready, turn.n(1, e + 1))
                        nc.scalar.activation(edge[e % 2][:], edge[e % 2][:], ACT.Exp, scale=-1.0).then_inc(e_ready, 1)
                        act.wait_ge(e_ready, turn.n(1, e + 1))
                        wait(act, h_done, turn.n(1, e + 1 - RING))
                        nc.scalar.copy(et_hi[e % RING][:], edge[e % 2][:]).then_inc(et_hi_ready, 1)
                    for rc, at in ((0, 3), (1, 7)):
                        if (c := turn.block(s, at)) is not None:
                            act.wait_ge(mask_ready, turn.blocks(RC, c * RC + rc + 1))
                            tile = turn.it * (2 * RC) + c * RC + rc
                            nc.scalar.activation(count_junk[:], bias_t[rc][:].rearrange("p c r -> p (c r)"), ACT.Copy, scale=-1.0 / BIG,
                                                 accum_out=masked_count[:, bass.ds(tile, 1)]).then_inc(counted, 1)
                            act.wait_ge(counted, turn.blocks(RC, c * RC + rc + 1))
                    if (c := turn.block(s, 9)) is not None:
                        act.wait_ge(g_done, turn.n(1, (c + 1) * JP))
                        wait(act, mixed, mixed_at(c - 1, 8))
                        nc.scalar.copy(pg[:, 0, :], bank[0][:, 0:GW])
                        nc.scalar.copy(pg[:, 1, :], bank[1][:, 0:GW]).then_inc(pg_copied, 1)
                    if (c := turn.block(s, 11)) is not None:
                        act.wait_ge(h_done, turn.n(1, (c + 1) * JP))
                        nc.scalar.copy(ph[:, 0, :], bank[2][:, 0:GW])
                        nc.scalar.copy(ph[:, 1, :], bank[3][:, 0:GW]).then_inc(ph_copied, 1)
                    if (c := turn.block(s, 13)) is not None:
                        act.wait_ge(mixed, mixed_at(c, 1))
                        nc.scalar.activation(gates[:, 1], gates[:, 0], ACT.Tanh, scale=0.5).then_inc(gate_tanh, 1)
                    if (c := turn.block(s, 15)) is not None:
                        act.wait_ge(mixed, mixed_at(c, 8))
                        nc.scalar.activation(mix[:, 1], mix[:, 0], ACT.Tanh, scale=0.5).then_inc(mix_tanh, 1)
                    if (c := turn.block(s, 17)) is not None:
                        act.wait_ge(mixed, mixed_at(c, 13))
                        nc.scalar.activation(rstd[:, 1, :], rstd[:, 0, :], ACT.Sqrt).then_inc(std_ready, 1)

            turns(act, body)

            for n in range(0, XT_SLOTS, 2):
                act.wait_ge(x1t_full, n + 1)
                nc.scalar.copy(xt_dst(xt, *xt_order()[n]), bank[n][:].rearrange("x (c p) -> x c p", c=4)).then_inc(x1t_ready, 1)

        @block.vector
        def _(dve):
            nc.vector.memset(ones[:], 1.0)
            nc.vector.memset(h_lo[:].bitcast(f32), 0.0)
            nc.vector.memset(h_hi[:, :, D + 1:GW].bitcast(f32), 0.0)
            nc.vector.memset(h_hi[:, :, D:D + 1].bitcast(f32), 1.0)
            for s, (kt, rc, ch) in enumerate(xt_order()):
                dve.wait_ge(slot_full, s + 1)
                nc.vector.tensor_copy(xt_dst(xt, kt, rc, ch), slot_bank[s][:].rearrange("x (c p) -> x c p", c=4)).then_inc(slot_free, 1)
            dve.wait_ge(in_w, 32)
            dve.wait_ge(in_small, 128)
            for kt in range(KT):
                for o, dst in ((0, wl[:, kt, :]), (D, proj[:, kt, GW + D:GW + D + 1])):
                    nc.vector.tensor_tensor_reduce(out=junk[:], in0=proj[:, kt, GW:GW + D], in1=a_bc[:, o:o + D], scale=1.0,
                                                   scalar=0.0, op0=ALU.mult, op1=ALU.add, accum_out=dst).then_inc(wl_ready, 1)
                    dve.wait_ge(wl_ready, 2 * kt + (o > 0) + 1)
            for kt in range(KT):
                nc.vector.tensor_scalar(wl_rep[:, kt, :], ones[:], wl[:, kt, :], None, ALU.mult).then_inc(wl_done, 1)
            for s in range(PROJ0, LEFT0):
                j, which = divmod(s - PROJ0, 2)
                dve.wait_ge(slot_hi, s - PROJ0 + 1)
                if which == 0:
                    nc.vector.tensor_tensor(g_lo[:, j, :], slot_bank[s][:, 0:GW], g_hi[:, j, :].bitcast(f32), ALU.subtract).then_inc(slot_free, 1)
                else:
                    nc.vector.tensor_copy(s_right[:, j:j + 1], slot_bank[s][:, D:D + 1])
                    nc.vector.tensor_tensor(h_lo[:, j, 0:D], slot_bank[s][:, 0:D], h_hi[:, j, 0:D].bitcast(f32), ALU.subtract).then_inc(slot_free, 1)
            for q in range(QCH):
                s = LEFT0 + q
                dve.wait_ge(slot_full, s + 1)
                rc, half = divmod(q, 2)
                nc.vector.tensor_copy(s_left[:, :, rc, half * 64:half * 64 + 64],
                                      slot_bank[s][:].rearrange("x (p c) -> x c p", c=C)).then_inc(slot_free, 1)
            dve.wait_ge(slot_full, SLOTS)
            nc.vector.tensor_tensor(gate_xi[:, :, :], slot_bank[SLOTS - 1][:, 0:2 * NT].rearrange("p (t o) -> p t o", o=2),
                                    gate_b[:].rearrange("p (u o) -> p u o", u=1).broadcast_to((P, NT, 2)), ALU.add).then_inc(slot_free, 1)
            dve.wait_ge(slot_free, SLOTS)

            def body(turn, steps):
                def scores(t):
                    par, jp = divmod(t, JP)
                    r, tr = t % RING, bank[4 + t % 4][:].rearrange("p (j i) -> p j i", j=2)
                    dve.wait_ge(at_hi_ready, turn.n(1, t + 1))
                    nc.vector.tensor_tensor(at_lo[r][:], tr, at_hi[r][:].bitcast(f32), ALU.subtract)
                    wait(dve, z_ready, turn.n(1, t))
                    nc.vector.tensor_scalar(off[:], tr, 0.0, BIG, ALU.is_equal, ALU.mult).then_inc(t_free, 1)
                    dve.wait_ge(t_free, turn.n(1, t + 1))
                    wait(dve, leaky_ready, turn.n(1, t))
                    for jj in range(2):
                        j = 2 * jp + jj
                        row = s_left[:, bass.ds(turn.it * 2 + par, 1)].rearrange("x o r p -> x (o r p)")
                        last = nc.vector.scalar_tensor_tensor(out=z[:, jj, :], in0=row, scalar=s_right[:, j:j + 1],
                                                              in1=off[:, jj, :], op0=ALU.add, op1=ALU.add)
                    last.then_inc(z_ready, 1)
                    dve.wait_ge(z_ready, turn.n(1, t + 1))
                    wait(dve, et_lo_ready, turn.n(1, t - 1))
                    nc.vector.scalar_tensor_tensor(out=edge[t % 2][:], in0=z[:], scalar=0.01, in1=z[:],
                                                   op0=ALU.mult, op1=ALU.max).then_inc(leaky_ready, 1)

                def mask(c, rc):
                    dve.wait_ge(adj_in[c % 2], turn.it * 16 + 16)
                    wait(dve, bias_stored[rc], turn.blocks(16, 16 * c))
                    src = adj_n[c % 2][:, rc, :].rearrange("p (r c) -> p c r", c=C)
                    nc.vector.tensor_scalar(bias_t[rc][:], src, 0.0, -BIG, ALU.is_equal, ALU.mult).then_inc(mask_ready, 1)

                def epilogue(c, part):
                    made = {0: 0, 1: 4, 2: 8, 3: 13}[part]
                    t0 = turn.it * 4 + c * 2

                    def link(ins):
                        nonlocal made
                        made += 1
                        ins.then_inc(mixed, 1)
                        dve.wait_ge(mixed, turn.blocks(LINKS, c * LINKS + made))

                    if part == 0:
                        dve.wait_ge(pg_copied, turn.blocks(1, c + 1))
                        dve.wait_ge(ph_copied, turn.blocks(1, c + 1))
                        link(nc.vector.tensor_tensor(gates[:, 0], pg[:, :, D:D + 2], gate_xi[:, bass.ds(t0, 2), :], ALU.add))
                        link(nc.vector.tensor_tensor(mix[:, 0], pg[:, :, 0:D], b_bc[:].rearrange("p (u d) -> p u d", u=1).broadcast_to((P, RC, D)), ALU.add))
                        link(nc.vector.tensor_scalar(den[:, 0, :].rearrange("p (r o) -> p r o", o=1), ph[:, :, D:D + 1], 1e-5, None, ALU.add))
                        link(nc.vector.reciprocal(den[:, 1, :], den[:, 0, :]))
                    if part == 1:
                        dve.wait_ge(gate_tanh, turn.blocks(1, c + 1))
                        link(nc.vector.tensor_scalar(gates[:, 2], gates[:, 1], 0.5, 0.5, ALU.mult, ALU.add))
                        link(nc.vector.tensor_tensor(gates[:, 0, :, 0:1], gates[:, 2, :, 0:1], den[:, 1, :].rearrange("p (r o) -> p r o", o=1), ALU.mult))
                        for rc in range(RC):
                            last = nc.vector.tensor_scalar(ph[:, rc, 0:D], ph[:, rc, 0:D], gates[:, 0, rc, 0:1], None, ALU.mult)
                        link(last)
                        for rc in range(RC):
                            last = nc.vector.scalar_tensor_tensor(out=mix[:, 0, rc, :], in0=mix[:, 0, rc, :], scalar=gates[:, 2, rc, 1:2],
                                                                  in1=ph[:, rc, 0:D], op0=ALU.mult, op1=ALU.add)
                        link(last)
                    if part == 2:
                        dve.wait_ge(mix_tanh, turn.blocks(1, c + 1))
                        link(nc.vector.tensor_scalar(mix[:, 1], mix[:, 1], 0.5, 0.5, ALU.mult, ALU.add))
                        xc = xn[:, :, bass.ds(turn.it * 2 + c, 1), :].rearrange("p r o d -> p r (o d)")
                        link(nc.vector.tensor_tensor(mix[:, 0], mix[:, 1], xc, ALU.add))
                        dve.sem_inc(dve_tick)
                        for rc in range(RC):
                            last = nc.vector.bn_stats(stats[:, rc, :], mix[:, 0, rc, :])
                        link(last)
                        dve.sem_inc(dve_tick)
                        for rc in range(RC):
                            last = nc.vector.bn_aggr(moments[:, rc, :], stats[:, rc, :])
                        link(last)
                        link(nc.vector.tensor_scalar(rstd[:, 0, :].rearrange("p (r o) -> p r o", o=1), moments[:, :, 1:2], g["LN_EPS"], None, ALU.add))
                    if part == 3:
                        dve.wait_ge(std_ready, turn.blocks(1, c + 1))
                        link(nc.vector.reciprocal(rstd[:, 2, :], rstd[:, 1, :]))
                        for rc in range(RC):
                            row = xn[:, rc, bass.ds(turn.it * 2 + c, 1), :].rearrange("p o d -> p (o d)")
                            last = nc.vector.tensor_scalar(row, mix[:, 0, rc, :], moments[:, rc, 0:1], rstd[:, 2, rc:rc + 1],
                                                           ALU.subtract, ALU.mult)
                        last.then_inc(x1_ready, 1)
                        assert made == LINKS

                for s in range(steps):
                    if (t := turn.step(s, 0)) is not None:
                        scores(t)
                    for rc, at in ((0, 2), (1, 6)):
                        if (c := turn.block(s, at)) is not None:
                            mask(c, rc)
                    for part in range(4):
                        if (c := turn.block(s, 12 + 2 * part)) is not None:
                            epilogue(c, part)

            turns(dve, body)

            for n in range(1, XT_SLOTS, 2):
                dve.wait_ge(x1t_full, n + 1)
                nc.vector.tensor_copy(xt_dst(xt, *xt_order()[n]), bank[n][:].rearrange("x (c p) -> x c p", c=4)).then_inc(x1t_ready, 1)


def layer1(nc, g):
    f32, f32r, ALU, ACT, AX = g["f32"], g["f32r"], g["ALU"], g["ACT"], g["AX"]
    N, D, HEADS, C, R, RC, KT, NT = (g[k] for k in ("N", "D", "HEADS", "C", "R", "RC", "KT", "NT"))
    bank, ident, masked_count = g["bank"], g["ident"], g["masked_count"]
    NB = N // BANK
    TPB = BANK // P
    QCH = N // BANK
    CH = D * C // BANK
    PROBS = TPB + 1
    RING = 3
    HALF_SCALE = D ** -0.5 / 2

    PROJ = 2 * CH
    SLOTS_H = 3 * PROJ + NT * QCH + NB * TPB // 2
    SPLITS_H = 3 * CH

    ctx = ExitStack()
    with ctx:
        def sb(name, shape, dt=f32):
            return ctx.enter_context(nc.sbuf_tensor("l1_" + name, shape, dt))

        def sem(name):
            return ctx.enter_context(nc.semaphore("l1_" + name))

        kt_hi, kt_lo = sb("kt_hi", [P, KT, N], f32r), sb("kt_lo", [P, KT, N], f32r)
        v_hi, v_lo = sb("v_hi", [P, NT, D], f32r), sb("v_lo", [P, NT, D], f32r)
        qt_hi, qt_lo = sb("qt_hi", [P, KT, BANK], f32r), sb("qt_lo", [P, KT, BANK], f32r)
        probs = sb("probs", [P, PROBS, N])
        pt_hi, pt_lo = ([sb(f"pt_{w}{i}", [P, BANK], f32r) for i in range(RING)] for w in ("hi", "lo"))
        ot_hi, ot_lo = sb("ot_hi", [P, KT, BANK], f32r), sb("ot_lo", [P, KT, BANK], f32r)
        w_raw = [sb(f"w_raw{i}", [P, KT, BANK]) for i in range(2)]
        w_hi, w_lo = ([sb(f"w_{w}{i}", [P, KT, BANK], f32r) for i in range(2)] for w in ("hi", "lo"))
        xh_raw, xh_hi, xh_lo = sb("xh_raw", [P, KT, R]), sb("xh_hi", [P, KT, R], f32r), sb("xh_lo", [P, KT, R], f32r)
        wo_raw, wo_hi, wo_lo = sb("wo_raw", [P, KT, D]), sb("wo_hi", [P, KT, D], f32r), sb("wo_lo", [P, KT, D], f32r)
        bias_t = [sb(f"bias_t{i}", [P, N]) for i in range(2)]
        y = sb("y", [P, NT, D])
        maxes = sb("maxes", [P, NT, QCH + 1])
        row_max = sb("row_max", [P, NT, 1])
        exp_bias = sb("exp_bias", [P, NT])
        den = sb("den", [P, NT])
        capped, masked_exp, masked_sum, rden = (sb(n, [P, NT]) for n in ("capped", "masked_exp", "masked_sum", "rden"))
        ref_mask = sb("ref_mask", [P, 1])
        stats = sb("stats", [P, NT, 6])
        mv = sb("mv", [P, NT, 2])
        rstd = sb("rstd", [P, 3, NT])

        pool_tick, dve_tick = sem("pool_tick"), sem("dve_tick")
        ready, w_in, x_in, wo_in = sem("ready"), [sem("w_in0"), sem("w_in1")], sem("xh_in"), sem("wo_in")
        bias_in = [sem("bias_in0"), sem("bias_in1")]
        w_hi_ready, w_split = sem("w_hi_ready"), sem("w_split")
        xh_hi_ready, xh_split, wo_hi_ready, wo_split = sem("xh_hi_ready"), sem("xh_split"), sem("wo_hi_ready"), sem("wo_split")
        slot_full, slot_hi, slot_free = sem("slot_full"), sem("slot_hi"), sem("slot_free")
        max_ready, scores_ready, probs_ready = sem("max_ready"), sem("scores_ready"), sem("probs_ready")
        pt_full, pt_hi_ready, pt_split, pt_used = sem("pt_full"), sem("pt_hi_ready"), sem("pt_split"), sem("pt_used")
        ot_full, ot_hi_ready, ot_split = sem("ot_full"), sem("ot_hi_ready"), sem("ot_split")
        capped_ready, masked_ready, den_step = sem("capped_ready"), sem("masked_ready"), sem("den_step")
        floor_step, summed = sem("floor_step"), sem("summed")
        x1_in, y_step, std_ready, normed, out_done = sem("x1_in"), sem("y_step"), sem("std_ready"), sem("normed"), sem("out_done")

        class Walk:
            PER_HEAD = dict(slot=SLOTS_H, proj=3 * PROJ, split=SPLITS_H, used=SPLITS_H, rows=1, head=1, tile=NT, block=NB, pt=NB * NT)

            def __init__(self):
                self.n = dict.fromkeys(self.PER_HEAD, 0)
                self.it = None
                self.out_slot = 0

            def at(self, what, k=0):
                here = self.n[what] + k
                return here if self.it is None else self.it * self.PER_HEAD[what] + here

            def past(self, what, k=1):
                self.n[what] += k

        def walk_heads(w, eng, start, rest, end):
            start()
            before = dict(w.n)
            with eng.Fori(0, HEADS - 1) as it:
                w.it = it
                rest()
            w.it = None
            for k, per in w.PER_HEAD.items():
                made = w.n[k] - before[k]
                assert made in (0, per), (k, made, per)
                w.n[k] += (HEADS - 2) * made
            w.out_slot += (HEADS - 2) * SLOTS_H
            end()

        def order(do, first):
            if first:
                do.rows()
                do.split()
                do.split()
            for j in range(CH):
                do.project("k", j)
                do.split()
            if not first:
                do.lead(NB - 1)
            do.project("q", 0)
            do.split()
            if not first:
                do.attend(NB - 1)
                do.project_out(NB - 1)
            do.out_weights()
            for t in range(TPB):
                do.scores(0, t)
            do.project("q", 1)
            do.split()
            for j in range(CH):
                do.project("v", j)
                do.split()
            for nb in range(1, NB):
                do.scores(nb, 0)
                do.attend(nb - 1)
                do.scores(nb, 1)
                if nb > 1:
                    do.split()
                if nb == NB - 1:
                    do.rows()
                do.scores(nb, 2)
                do.scores(nb, 3)
                if nb + 1 < NB:
                    do.project("q", nb + 1)
                do.project_out(nb - 1)

        def last_part(do):
            do.lead(NB - 1)
            do.attend(NB - 1)
            do.project_out(NB - 1)

        WEIGHTS = ["k"] * CH + ["q"] * 2 + ["v"] * CH + ["q"] * 2
        CHUNK = list(range(CH)) + [0, 1] + list(range(CH)) + [2, 3]
        src_of = {"k": g["wk"], "q": g["wq"], "v": g["wv"]}

        block = ctx.enter_context(nc.Block())

        @block.gpsimd
        def _(pool):
            def load_w(i, h):
                v = src_of[WEIGHTS[i]].rearrange("(k p) n -> p k n", p=P)
                if h is None:
                    if i >= 2:
                        pool.wait_ge(w_split, i - 1)
                else:
                    pool.wait_ge(w_split, h * SPLITS_H + i - 1)
                    pool.sem_inc(pool_tick)
                pool.dma_start(w_raw[i % 2][:], v[:, :, CHUNK[i] * BANK:(CHUNK[i] + 1) * BANK]).then_inc(w_in[i % 2], 16)

            pool.dma_start(xh_raw[:], g["x1t_d"][:, :, 0:R]).then_inc(x_in, 16)
            load_w(0, None)
            load_w(1, None)
            pool.dma_start(wo_raw[:], g["wout"][0:D, :].rearrange("(k p) n -> p k n", p=P)).then_inc(wo_in, 16)
            for i in range(2, SPLITS_H):
                load_w(i, None)
            with pool.Fori(1, HEADS) as h:
                pool.wait_ge(xh_split, h)
                pool.sem_inc(pool_tick)
                pool.dma_start(xh_raw[:], g["x1t_d"][:, :, bass.ds(h * R, R)]).then_inc(x_in, 16)
                load_w(0, h)
                load_w(1, h)
                pool.wait_ge(wo_split, h)
                pool.sem_inc(pool_tick)
                pool.dma_start(wo_raw[:], g["wout"][bass.ds(h * D, D), :].rearrange("(k p) n -> p k n", p=P)).then_inc(wo_in, 16)
                for i in range(2, SPLITS_H):
                    load_w(i, h)
            pool.wait_ge(xh_split, HEADS)
            pool.dma_start(xh_raw[:], g["x1t_d"][:, :, 0:R]).then_inc(x_in, 16)
            for i in range(2):
                pool.wait_ge(w_split, HEADS * SPLITS_H + i - 1)
                pool.dma_start(w_raw[i][:], src_of["k"].rearrange("(k p) n -> p k n", p=P)[:, :, i * BANK:(i + 1) * BANK]).then_inc(w_in[i], 16)
            pool.wait_ge(x_in, 16 * (HEADS + 1))

        @block.sync
        def _(sp):
            sp.dma_start(bias_t[0][:], g["bias_d"][0]).then_inc(bias_in[0], 16)
            sp.dma_start(bias_t[1][:], g["bias_d"][1]).then_inc(bias_in[1], 16)
            for t in range(2, NT):
                sp.wait_ge(max_ready, t - 1)
                sp.dma_start(bias_t[t % 2][:], g["bias_d"][t]).then_inc(bias_in[t % 2], 16)
            with sp.Fori(1, HEADS) as h:
                for t in range(NT):
                    sp.wait_ge(max_ready, h * NT + t - 1)
                    sp.dma_start(bias_t[t % 2][:], g["bias_d"][t]).then_inc(bias_in[t % 2], 16)
            sp.wait_ge(pt_full, HEADS * NB * NT)
            sp.dma_start(probs[:, 0:2, :].rearrange("p a n -> p (a n)"), g["x1_d"]).then_inc(x1_in, 16)
            out_v = g["out"].rearrange("(rc p c) d -> p c rc d", rc=RC, p=P)
            for c in range(C):
                sp.wait_ge(normed, RC * (c + 1))
                sp.dma_start(out_v[:, c], y[:, c * RC:(c + 1) * RC, :]).then_inc(out_done, 16)
            sp.wait_ge(out_done, 16 * C)

        @block.tensor
        def _(pe):
            w = Walk()

            def take():
                if w.it is not None or w.n["slot"] >= 4:
                    pe.wait_ge(slot_free, w.at("slot", -3))
                b = bank[w.n["slot"] % 4]
                w.past("slot")
                return b

            def three(o, a_hi, a_lo, b_hi, b_lo, start, stop):
                nc.tensor.matmul(o, a_hi, b_hi, start=start, stop=False)
                nc.tensor.matmul(o, a_hi, b_lo, start=False, stop=False)
                return nc.tensor.matmul(o, a_lo, b_hi, start=False, stop=stop)

            class Do:
                def rows(self):
                    pass

                def split(self):
                    pass

                def out_weights(self):
                    self.wo_lag = 0

                def project(self, which, j):
                    if which == "k" and j == 0:
                        w.past("head")
                        pe.wait_ge(xh_split, w.at("head"))
                        self.wo_lag = -1
                    wh, wl = w_hi[w.n["used"] % 2], w_lo[w.n["used"] % 2]
                    w.past("used")
                    pe.wait_ge(w_split, w.at("used"))
                    for i in range(2):
                        b = take()
                        if which == "v":
                            for k in range(KT):
                                rows = slice(i * P, (i + 1) * P)
                                last = three(b[:], xh_hi[:, k, rows], xh_lo[:, k, rows], wh[:, k, :], wl[:, k, :], k == 0, k == KT - 1)
                        else:
                            for ci in range(2):
                                for k in range(KT):
                                    cols = slice(ci * D + i * P, ci * D + (i + 1) * P)
                                    last = three(b[:, ci * R:(ci + 1) * R], wh[:, k, cols], wl[:, k, cols], xh_hi[:, k, :], xh_lo[:, k, :],
                                                 k == 0, k == KT - 1)
                        last.then_inc(slot_full, 1)
                    if which == "q":
                        self.q_slot = w.n["slot"]

                def scores(self, nb, t):
                    if t == 0:
                        pe.wait_ge(slot_free, w.at("slot", self.q_slot - w.n["slot"]))
                    for q in range(QCH):
                        if t == 0 and nb > 0 and q == QCH - 1:
                            self.lead(nb - 1)
                        b = take()
                        for k in range(KT):
                            rows, keys = slice(t * P, (t + 1) * P), slice(q * BANK, (q + 1) * BANK)
                            last = three(b[:], qt_hi[:, k, rows], qt_lo[:, k, rows], kt_hi[:, k, keys], kt_lo[:, k, keys], k == 0, k == KT - 1)
                        last.then_inc(slot_full, 1)

                def transposes(self, nb, k):
                    if w.it is not None or w.n["pt"] >= 2:
                        pe.wait_ge(pt_split, w.at("pt", -1))
                    for t in range(TPB):
                        last = nc.tensor.transpose(bank[4 + k % 2][:, t * P:(t + 1) * P],
                                                   probs[:, (nb * TPB + t) % PROBS, k * P:(k + 1) * P], ident[:])
                    last.then_inc(pt_full, 1)
                    w.past("pt")

                def lead(self, nb):
                    w.past("block")
                    pe.wait_ge(probs_ready, w.at("block") * TPB)
                    self.transposes(nb, 0)
                    self.transposes(nb, 1)

                def attend(self, nb):
                    for k in range(NT):
                        if k + 2 < NT:
                            self.transposes(nb, k + 2)
                        behind = min(k + 3, NT)
                        pe.wait_ge(pt_split, w.at("pt", k + 1 - behind))
                        if k == 0 and (w.it is not None or w.n["block"] > 1):
                            pe.wait_ge(ot_split, w.at("block", -1))
                        ph, pl = pt_hi[(nb * NT + k) % RING], pt_lo[(nb * NT + k) % RING]
                        for d in range(KT):
                            cols = slice(d * P, (d + 1) * P)
                            last = three(bank[6 + d][:], v_hi[:, k, cols], v_lo[:, k, cols], ph[:], pl[:], k == 0, k == NT - 1)
                        last.then_inc(pt_used, 1)

                def project_out(self, nb):
                    pe.wait_ge(ot_split, w.at("block"))
                    pe.wait_ge(wo_split, w.at("head", self.wo_lag))
                    for pair in range(TPB // 2):
                        b = take()
                        for i in range(2):
                            t = 2 * pair + i
                            for k in range(KT):
                                rows = slice(t * P, (t + 1) * P)
                                last = three(b[:, i * D:(i + 1) * D], ot_hi[:, k, rows], ot_lo[:, k, rows], wo_hi[:, k, :], wo_lo[:, k, :],
                                             k == 0, k == KT - 1)
                        last.then_inc(slot_full, 1)

            do = Do()

            walk_heads(w, pe, lambda: order(do, True), lambda: order(do, False), lambda: last_part(do))

        @block.scalar
        def _(act):
            w = Walk()

            class Do:
                def split(self):
                    i = w.n["split"]
                    w.past("split")
                    loads = 16 * (i // 2 + 1)
                    act.wait_ge(w_in[i % 2], loads if w.it is None else w.it * (8 * SPLITS_H) + loads)
                    if w.it is not None or w.n["slot"]:
                        act.wait_ge(slot_full, w.at("slot"))
                    nc.scalar.copy(w_hi[i % 2][:], w_raw[i % 2][:]).then_inc(w_hi_ready, 1)
                    self.exponentials_left()

                def rows(self):
                    w.past("rows")
                    act.wait_ge(x_in, 16 * w.at("rows"))
                    if w.it is not None or w.n["slot"]:
                        act.wait_ge(slot_full, w.at("slot"))
                    nc.scalar.copy(xh_hi[:], xh_raw[:]).then_inc(xh_hi_ready, 1)

                def out_weights(self):
                    w.past("head")
                    act.wait_ge(wo_in, 16 * w.at("head"))
                    if w.it is not None:
                        act.wait_ge(slot_full, w.at("slot"))
                    nc.scalar.copy(wo_hi[:], wo_raw[:]).then_inc(wo_hi_ready, 1)

                def project(self, which, j):
                    for i in range(2):
                        b = bank[w.n["slot"] % 4]
                        w.past("slot")
                        w.past("proj")
                        act.wait_ge(slot_full, w.at("slot"))
                        if which == "k":
                            nc.scalar.copy(kt_hi[:, i, j * BANK:(j + 1) * BANK], b[:]).then_inc(slot_hi, 1)
                        elif which == "q":
                            nc.scalar.mul(qt_hi[:, i, :], b[:], HALF_SCALE).then_inc(slot_hi, 1)
                        else:
                            dst = v_hi[:, 4 * j:4 * j + 4, :].rearrange("p (c r) d -> p r c d", r=RC)[:, i]
                            nc.scalar.copy(dst, b[:].rearrange("p (c d) -> p c d", c=2)).then_inc(slot_hi, 1)

                pending = None
                late = None

                def exponentials_left(self):
                    if self.late:
                        self.exponentials(*self.late)
                        self.late = None

                def scores(self, nb, t):
                    w.past("slot", QCH)
                    w.past("tile")
                    if t == 0 and nb > 0:
                        self.lead(nb - 1)
                        self.pending = (nb, t, w.at("tile"))
                    elif t == TPB - 1:
                        self.late = (nb, t, w.at("tile"))
                    else:
                        self.exponentials(nb, t, w.at("tile"))

                def exponentials(self, nb, t, tile):
                    n = nb * TPB + t
                    p = probs[:, n % PROBS, :]
                    act.wait_ge(scores_ready, tile)
                    nc.scalar.activation(p, p, ACT.Exp, bias=exp_bias[:, n:n + 1], scale=2.0, accum_out=den[:, n:n + 1]).then_inc(probs_ready, 1)

                def transposed(self, nb, k):
                    w.past("pt")
                    act.wait_ge(pt_full, w.at("pt"))
                    if w.it is not None or w.n["pt"] > RING:
                        act.wait_ge(pt_used, w.at("pt", -RING))
                    nc.scalar.copy(pt_hi[(nb * NT + k) % RING][:], bank[4 + k % 2][:]).then_inc(pt_hi_ready, 1)

                def lead(self, nb):
                    w.past("block")
                    self.transposed(nb, 0)
                    self.transposed(nb, 1)

                def attend(self, nb):
                    for k in range(2, NT):
                        self.transposed(nb, k)
                        if k == 2 and self.pending:
                            self.exponentials(*self.pending)
                            self.pending = None
                    act.wait_ge(pt_used, w.at("pt"))
                    if w.it is not None or w.n["block"] > 1:
                        act.wait_ge(slot_full, w.at("slot", w.out_slot - w.n["slot"]))
                    for d in range(KT):
                        nc.scalar.copy(ot_hi[:, d, :], bank[6 + d][:]).then_inc(ot_hi_ready, 1)
                    cols = slice(nb * TPB, (nb + 1) * TPB)
                    act.wait_ge(capped_ready, w.at("block"))
                    nc.scalar.activation(masked_exp[:, cols], capped[:, cols], ACT.Exp, bias=ref_mask[:, 0:1]).then_inc(masked_ready, 1)

                def project_out(self, nb):
                    self.exponentials_left()
                    w.past("slot", TPB // 2)
                    w.out_slot = w.n["slot"]

            do = Do()

            act.wait_ge(ready, 1)
            walk_heads(w, act, lambda: order(do, True), lambda: order(do, False), lambda: last_part(do))
            act.wait_ge(y_step, 2)
            nc.scalar.activation(rstd[:, 1, :], rstd[:, 0, :], ACT.Sqrt).then_inc(std_ready, 1)

        @block.vector
        def _(dve):
            w = Walk()

            class Do:
                def lo(self, dst, src, hi):
                    return nc.vector.tensor_tensor(dst, src, hi.bitcast(f32), ALU.subtract)

                def split(self):
                    i = w.n["split"]
                    w.past("split")
                    dve.wait_ge(w_hi_ready, w.at("split"))
                    self.lo(w_lo[i % 2][:], w_raw[i % 2][:], w_hi[i % 2][:]).then_inc(w_split, 1)

                def rows(self):
                    w.past("rows")
                    dve.wait_ge(xh_hi_ready, w.at("rows"))
                    self.lo(xh_lo[:], xh_raw[:], xh_hi[:]).then_inc(xh_split, 1)

                def out_weights(self):
                    w.past("head")
                    dve.wait_ge(wo_hi_ready, w.at("head"))
                    self.lo(wo_lo[:], wo_raw[:], wo_hi[:]).then_inc(wo_split, 1)
                    if w.it is None:
                        nc.vector.memset(y[:], 0.0)

                def project(self, which, j):
                    for i in range(2):
                        b = bank[w.n["slot"] % 4]
                        w.past("slot")
                        w.past("proj")
                        dve.wait_ge(slot_hi, w.at("proj"))
                        if which == "k":
                            keys = slice(j * BANK, (j + 1) * BANK)
                            last = self.lo(kt_lo[:, i, keys], b[:], kt_hi[:, i, keys])
                        elif which == "q":
                            last = nc.vector.scalar_tensor_tensor(out=qt_lo[:, i, :], in0=b[:], scalar=HALF_SCALE, in1=qt_hi[:, i, :].bitcast(f32),
                                                                  op0=ALU.mult, op1=ALU.subtract)
                        else:
                            def part(t):
                                return t[:, 4 * j:4 * j + 4, :].rearrange("p (c r) d -> p r c d", r=RC)[:, i]
                            last = self.lo(part(v_lo), b[:].rearrange("p (c d) -> p c d", c=2), part(v_hi))
                        last.then_inc(slot_free, 1)

                def scores(self, nb, t):
                    n = nb * TPB + t
                    w.past("tile")
                    dve.wait_ge(bias_in[n % 2], self.bias_loads(n))
                    if n >= PROBS:
                        dve.wait_ge(pt_full, w.at("pt"))
                    for q in range(QCH):
                        if t == 0 and nb > 0 and q == QCH - 1:
                            self.lead(nb - 1)
                        b = bank[w.n["slot"] % 4]
                        w.past("slot")
                        keys = slice(q * BANK, (q + 1) * BANK)
                        dve.wait_ge(slot_full, w.at("slot"))
                        dve.sem_inc(dve_tick)
                        nc.vector.tensor_tensor_reduce(out=probs[:, n % PROBS, keys], in0=b[:], in1=bias_t[n % 2][:, keys], scale=1.0, scalar=LOWEST,
                                                       op0=ALU.add, op1=ALU.max, accum_out=maxes[:, n, q:q + 1]).then_inc(slot_free, 1)
                    dve.wait_ge(slot_free, w.at("slot"))
                    nc.vector.tensor_reduce(out=row_max[:, n, :], in_=maxes[:, n, :], axis=AX.X, op=ALU.max).then_inc(max_ready, 1)
                    dve.wait_ge(max_ready, w.at("tile"))
                    nc.vector.tensor_scalar(exp_bias[:, n:n + 1], row_max[:, n, :], -2.0, None, ALU.mult).then_inc(scores_ready, 1)
                    if t == TPB - 1:
                        cols = slice(nb * TPB, (nb + 1) * TPB)
                        dve.wait_ge(scores_ready, w.at("tile"))
                        nc.vector.tensor_scalar(capped[:, cols], exp_bias[:, cols], -REF_MASK, None, ALU.min).then_inc(capped_ready, 1)

                def bias_loads(self, n):
                    k = 16 * ((w.n["tile"] - 1) // NT) * (NT // 2) + 16 * (n // 2 + 1)
                    return k if w.it is None else w.it * (8 * NT) + k

                def transposed(self, nb, k):
                    w.past("pt")
                    r = (nb * NT + k) % RING
                    dve.wait_ge(pt_hi_ready, w.at("pt"))
                    self.lo(pt_lo[r][:], bank[4 + k % 2][:], pt_hi[r][:]).then_inc(pt_split, 1)

                def lead(self, nb):
                    w.past("block")
                    self.transposed(nb, 0)
                    self.transposed(nb, 1)

                def attend(self, nb):
                    for k in range(2, NT):
                        self.transposed(nb, k)
                    dve.wait_ge(ot_hi_ready, w.at("block") * KT)
                    for d in range(KT):
                        last = self.lo(ot_lo[:, d, :], bank[6 + d][:], ot_hi[:, d, :])
                    last.then_inc(ot_split, 1)
                    cols = slice(nb * TPB, (nb + 1) * TPB)
                    dve.wait_ge(masked_ready, w.at("block"))
                    nc.vector.tensor_tensor(masked_sum[:, cols], masked_exp[:, cols], masked_count[:, cols], ALU.mult).then_inc(den_step, 1)
                    dve.wait_ge(den_step, w.at("block") * 3 - 2)
                    nc.vector.tensor_tensor(masked_sum[:, cols], masked_sum[:, cols], den[:, cols], ALU.add).then_inc(den_step, 1)
                    dve.wait_ge(den_step, w.at("block") * 3 - 1)
                    nc.vector.reciprocal(rden[:, cols], masked_sum[:, cols]).then_inc(den_step, 1)

                def project_out(self, nb):
                    dve.wait_ge(den_step, w.at("block") * 3)
                    for pair in range(TPB // 2):
                        b = bank[w.n["slot"] % 4]
                        w.past("slot")
                        dve.wait_ge(slot_full, w.at("slot"))
                        for i in range(2):
                            n = nb * TPB + 2 * pair + i
                            last = nc.vector.scalar_tensor_tensor(out=y[:, n, :], in0=b[:, i * D:(i + 1) * D], scalar=rden[:, n:n + 1],
                                                                  in1=y[:, n, :], op0=ALU.mult, op1=ALU.add)
                        last.then_inc(slot_free, 1)

            do = Do()

            nc.vector.memset(ref_mask[:], REF_MASK).then_inc(y_step, 1)
            dve.wait_ge(y_step, 1)
            floor = maxes[:, :, QCH:QCH + 1]
            nc.vector.tensor_scalar(row_max[:], masked_count[:].rearrange("p (t o) -> p t o", o=1), 0.0, -LOWEST, ALU.is_equal, ALU.mult).then_inc(floor_step, 1)
            dve.wait_ge(floor_step, 1)
            nc.vector.tensor_scalar(floor, row_max[:], -1.0, REF_MASK / 2, ALU.mult, ALU.add).then_inc(ready, 1)
            dve.wait_ge(ready, 1)
            walk_heads(w, dve, lambda: order(do, True), lambda: order(do, False), lambda: last_part(do))

            dve.wait_ge(x1_in, 16)
            dve.wait_ge(slot_free, HEADS * SLOTS_H)
            x1 = probs[:, 0:2, :].rearrange("p a (c d) -> p a c d", d=D)
            for rc in range(RC):
                yc = y[:].rearrange("p (c r) d -> p r c d", r=RC)[:, rc]
                last = nc.vector.tensor_tensor(yc, yc, x1[:, rc], ALU.add)
            last.then_inc(summed, 1)
            dve.wait_ge(summed, 1)
            for t in range(NT):
                last = nc.vector.bn_stats(stats[:, t, :], y[:, t, :])
            last.then_inc(summed, 1)
            dve.wait_ge(summed, 2)
            for t in range(NT):
                last = nc.vector.bn_aggr(mv[:, t, :], stats[:, t, :])
            last.then_inc(summed, 1)
            dve.wait_ge(summed, 3)
            nc.vector.tensor_scalar(rstd[:, 0, :].rearrange("p (t o) -> p t o", o=1), mv[:, :, 1:2], g["LN_EPS"], None, ALU.add).then_inc(y_step, 1)
            dve.wait_ge(std_ready, 1)
            nc.vector.reciprocal(rstd[:, 2, :], rstd[:, 1, :]).then_inc(summed, 1)
            dve.wait_ge(summed, 4)
            for t in range(NT):
                nc.vector.tensor_scalar(y[:, t, :], y[:, t, :], mv[:, t, 0:1], rstd[:, 2, t:t + 1], ALU.subtract,
                                        ALU.mult).then_inc(normed, 1)


_INS = ["x", "adj", "L0_gnn_W_sa", "L0_gnn_a_sa", "L0_gnn_W_gcnb", "L0_gnn_b_gcnb", "L0_gnn_Wa", "L0_gnn_ba",
        "L0_gnn_Wb", "L0_gnn_bb", "L1_gnn_Wq", "L1_gnn_Wk", "L1_gnn_Wv", "L1_gnn_Wout"]


def kernel(**inputs):
    import numpy as _np
    import concourse.bacc as _bacc
    from concourse import mybir as _mybir
    from concourse.bass_utils import run_bass_kernel_spmd as _run

    nc = _bacc.Bacc("TRN2", target_bir_lowering=False, num_devices=1)
    arrays, args = {}, []
    for name in _INS:
        a = _np.ascontiguousarray(inputs[name])
        arrays[f"in_{name}_dram"] = a
        args.append(nc.dram_tensor(f"in_{name}_dram", a.shape, _mybir.dt.from_np(a.dtype), kind="ExternalInput").ap())
    args.append(nc.dram_tensor("out_0_dram", (2048, 256), _mybir.dt.float32, kind="ExternalOutput").ap())
    gnn_two_layers(nc, *args)
    r = _run(nc, [arrays], core_ids=[0])
    return r.results[0]["out_0_dram"]
```

```python
import concourse.bass as bass
from concourse import mybir
from contextlib import ExitStack

P = 128
BANK = 512
BIG = float(2 ** 100)
REF_MASK = -1.0e6
LOWEST = -3.0e38


def gnn_two_layers(nc, x, adj, w_sa, a_sa, w_gcnb, b_gcnb, wa, ba, wb, bb, wq, wk, wv, wout, out):
    f32, f32r = mybir.dt.float32, mybir.dt.float32r
    ALU, ACT, AX = mybir.AluOpType, mybir.ActivationFunctionType, mybir.AxisListType

    N, D = x.shape
    HEADS = wq.shape[1] // D
    C = HEADS
    R = N // C
    KT = D // P
    RC = R // P
    NT = N // P
    QCH = N // BANK
    LN_EPS = 1e-5

    bias_d = nc.dram_tensor("bias_scratch", (NT, P, N), f32, kind="Internal").ap()
    x1t_d = nc.dram_tensor("x1t_scratch", (P, KT, N), f32, kind="Internal").ap()

    whole = ExitStack()
    with whole:
        bank = [whole.enter_context(nc.psum_tensor(f"bank{i}", [P, BANK], f32)) for i in range(8)]

        def keep(name, shape, dt=f32):
            return whole.enter_context(nc.sbuf_tensor(name, shape, dt))

        ident = keep("ident", [P, P])
        masked_count = keep("masked_count", [P, NT])
        x1 = keep("x1", [P, NT, D])
        xt = keep("xt", [P, KT, N])
        w_raw = [keep(f"w_raw{i}", [P, KT, BANK]) for i in range(2)]
        wo_raw = keep("wo_raw", [P, KT, D])
        wo_first = whole.enter_context(nc.semaphore("wo_first"))
        w_first = [whole.enter_context(nc.semaphore(f"w_first{i}")) for i in range(2)]
        layer0(nc, locals())
        layer1(nc, locals())




def layer0(nc, g):
    f32, f32r, ALU, ACT = g["f32"], g["f32r"], g["ALU"], g["ACT"]
    N, D, C, RC, KT, NT, QCH = (g[k] for k in ("N", "D", "C", "RC", "KT", "NT", "QCH"))
    bank, ident, masked_count = g["bank"], g["ident"], g["masked_count"]
    GW = D + 2
    HW = D + 2
    RING = 4
    JP = NT // 2
    TURN = 2 * JP
    IB = RC * P
    ADDS = 4
    LEAST = -8872.0
    LINKS = 10

    ctx = ExitStack()
    with ctx:
        def sb(name, shape, dt=f32):
            return ctx.enter_context(nc.sbuf_tensor("l0_" + name, shape, dt))

        def sem(name):
            return ctx.enter_context(nc.semaphore("l0_" + name))

        xn = g["x1"][:].rearrange("p (c r) d -> p r c d", r=RC)
        xt = g["xt"]
        b_bc = sb("b_bc", [P, D])
        gate_b = sb("gate_b", [P, 2])
        g_hi, g_lo = sb("g_hi", [P, NT, GW], f32r), sb("g_lo", [P, NT, GW], f32r)
        h_hi, h_lo = sb("h_hi", [P, NT, GW], f32r), sb("h_lo", [P, NT, GW], f32r)
        s_right = sb("s_right", [P, NT])
        between = xt[:].rearrange("p k n -> p (k n)")
        s_left = between[:, 0:N].rearrange("p (c r x) -> p c r x", c=C, r=RC)
        gate_xi = sb("gate_xi", [P, NT, 2])
        adj_n0 = sb("adj_n0", [P, RC, N])

        with ExitStack() as start:
            def early(name, shape, dt=f32):
                return start.enter_context(nc.sbuf_tensor("start_" + name, shape, dt))

            xt_hi, xt_lo = early("xt_hi", [P, KT, N], f32r), early("xt_lo", [P, KT, N], f32r)
            proj = early("proj", [P, KT, GW + HW])
            proj_hi, proj_lo = early("proj_hi", [P, KT, GW + HW], f32r), early("proj_lo", [P, KT, GW + HW], f32r)
            a_bc = early("a_bc", [P, 2 * D])
            gate_w = early("gate_w", [P, 2, D])
            wl, wl_rep = early("wl", [P, KT, 1]), early("wl_rep", [P, KT, P])
            wl_hi, wl_lo = early("wl_hi", [P, KT, P], f32r), early("wl_lo", [P, KT, P], f32r)
            ones, junk = early("ones", [P, P]), early("junk", [P, D])

        adj_n = [adj_n0, sb("adj_n1", [P, RC, N])]
        at_hi, at_lo = ([sb(f"at_{w}{i}", [P, 2, IB], f32r) for i in range(RING)] for w in ("hi", "lo"))
        et_hi, et_lo = ([sb(f"et_{w}{i}", [P, 2, IB], f32r) for i in range(RING)] for w in ("hi", "lo"))
        edge = [between[:, N + i * 2 * IB:N + (i + 1) * 2 * IB].rearrange("p (j i) -> p j i", j=2) for i in range(RING)]
        weight = [sb(f"weight{i}", [P, 2, IB]) for i in range(RING)]
        bias_t = [sb(f"bias_t{i}", [P, C, N // C]) for i in range(RC)]
        count_junk = sb("count_junk", [P, N], mybir.dt.uint8)
        pg, ph = sb("pg", [P, RC, GW]), sb("ph", [P, RC, GW])
        gates = sb("gates", [P, 3, RC, 2])
        den = sb("den", [P, 2, RC])
        pg_b, mix = sb("pg_b", [P, RC, D]), sb("mix", [P, RC, D])
        stats = sb("stats", [P, RC, 6])
        moments = sb("moments", [P, RC, 2])
        rstd = sb("rstd", [P, 3, RC])

        dve_tick, sp_tick = sem("dve_tick"), sem("sp_tick")
        ident_ready, in_x, in_w, in_small = sem("ident_ready"), [sem(f"in_x{i}") for i in range(4)], sem("in_w"), sem("in_small")
        wl_ready, wl_done, proj_hi_ready, proj_split = sem("wl_ready"), sem("wl_done"), sem("proj_hi_ready"), sem("proj_split")
        zeroed, gate_ready = sem("zeroed"), sem("gate_ready")
        slot_full, slot_hi, slot_free = sem("slot_full"), sem("slot_hi"), sem("slot_free")
        adj_in = [sem(f"adj_in{i}") for i in range(2)]
        t_full, at_hi_ready, e_masked = sem("t_full"), sem("at_hi_ready"), sem("e_masked")
        z_ready, leaky_ready, exp_ready, at_lo_ready, et_hi_ready, et_lo_ready = (
            sem("z_ready"), sem("leaky_ready"), sem("exp_ready"), sem("at_lo_ready"), sem("et_hi_ready"), sem("et_lo_ready"))
        g_done, h_done = sem("g_done"), sem("h_done")
        pg_copied, ph_copied = sem("pg_copied"), sem("ph_copied")
        mask_ready, counted, bias_added = sem("mask_ready"), sem("counted"), sem("bias_added")
        bias_stored = [sem(f"bias_stored{i}") for i in range(RC)]
        mixed, gate_tanh, b_added, ph_scaled = sem("mixed"), sem("gate_tanh"), sem("b_added"), sem("ph_scaled")
        mix_act, std_ready, rstd_ready = sem("mix_act"), sem("std_ready"), sem("rstd_ready")
        x1_ready, x1t_full, x1t_ready = (sem("x1_ready"), sem("x1t_full"), sem("x1t_ready"))

        adj_v = g["adj"].rearrange("(rc p c) m -> c p rc m", rc=RC, p=P)
        XT_SLOTS = KT * RC * 2
        PROJ0 = XT_SLOTS
        LEFT0 = PROJ0 + 2 * NT
        SLOTS = LEFT0 + QCH
        slot_bank = [bank[4 + i % 4] for i in range(SLOTS)]

        def xt_order():
            return [(kt, rc, ch) for rc in range(RC) for ch in range(2) for kt in range(KT)]

        def x1t_order():
            return [(kt, rc, ch) for ch in range(2) for rc in range(RC) for kt in range(KT)]

        def x1t_bank(n):
            return bank[(n + 4) % 8]

        def xt_dst(t, kt, rc, ch):
            v = t[:, kt, rc * P * C:(rc + 1) * P * C].rearrange("x (p c) -> x c p", c=C)
            return v[:, 4 * ch:4 * ch + 4, :]

        class Turn:
            def __init__(self, kind, it):
                self.kind, self.it = kind, it

            def live(self, back):
                return {"first": back >= 0, "loop": True, "drain": back < 0}[self.kind]

            def step(self, s, lag):
                return s - lag if self.live(s - lag) else None

            def block(self, s, at):
                b, m = divmod(s - at, JP)
                return b if m == 0 and self.live(b) else None

            def n(self, per_step, k):
                return self.it * (per_step * TURN) + k

            def blocks(self, per_block, k):
                return self.it * (per_block * 2) + k

        def turns(eng, body):
            body(Turn("first", 0), TURN)
            with eng.Fori(1, C // 2) as it:
                body(Turn("loop", it), TURN)
            body(Turn("drain", C // 2), JP + 8)

        def wait(eng, s, value):
            if not (isinstance(value, int) and value <= 0):
                eng.wait_ge(s, value)

        block = ctx.enter_context(nc.Block())

        @block.sync
        def _(sp):
            xv = g["x"].rearrange("(rc p c) d -> p rc c d", rc=RC, p=P)
            for i in (0, 2):
                rc, ch = divmod(i, 2)
                sp.dma_start(xn[:, rc, 4 * ch:4 * ch + 4, :], xv[:, rc, 4 * ch:4 * ch + 4, :]).then_inc(in_x[i], 16)
            sp.dma_start(proj[:, :, 0:D], g["w_gcnb"].rearrange("(k p) n -> p k n", p=P)).then_inc(in_w, 16)
            sp.dma_start(proj[:, :, GW:GW + D], g["w_sa"].rearrange("(k p) n -> p k n", p=P)).then_inc(in_w, 16)
            sp.wait_ge(in_w, 32)
            sp.wait_ge(in_small, 128)
            sp.dma_start(adj_n[0][:], adj_v[0]).then_inc(adj_in[0], 16)
            sp.wait_ge(slot_full, SLOTS)
            sp.dma_start(adj_n[1][:], adj_v[1]).then_inc(adj_in[1], 16)

            def store(c, tile, rc):
                sp.wait_ge(bias_added, c * (ADDS * RC) + ADDS * (rc + 1))
                sp.sem_inc(sp_tick)
                sp.dma_start(g["bias_d"][tile].rearrange("o p n -> (o p) n"),
                             bias_t[rc][:].rearrange("p c r -> p (c r)")).then_inc(bias_stored[rc], 16)

            with sp.Fori(0, C // 2 - 1) as it:
                for par in range(2):
                    for rc in range(RC):
                        store(it * 2 + par, bass.ds(it * 4 + par * RC + rc, 1), rc)
                    sp.wait_ge(t_full, it * TURN + (par + 1) * JP)
                    sp.sem_inc(sp_tick)
                    sp.dma_start(adj_n[par][:], adj_v[bass.ds(it * 2 + 2 + par, 1)].rearrange(
                        "o p rc m -> (o p) rc m")).then_inc(adj_in[par], 16)
            for i in range(2):
                sp.dma_start(g["w_raw"][i][:], g["wk"].rearrange("(k p) n -> p k n", p=P)[:, :, i * BANK:(i + 1) * BANK]).then_inc(g["w_first"][i], 16)
            sp.dma_start(g["wo_raw"][:], g["wout"][0:D, :].rearrange("(k p) n -> p k n", p=P)).then_inc(g["wo_first"], 16)
            for c in (C - 2, C - 1):
                for rc in range(RC):
                    store(c, slice(c * RC + rc, c * RC + rc + 1), rc)
            for rc in range(RC):
                sp.wait_ge(bias_stored[rc], 16 * C)

        @block.gpsimd
        def _(pool):
            nc.gpsimd.memset(ident[:], 0.0).then_inc(ident_ready, 1)
            pool.wait_ge(ident_ready, 1)
            nc.gpsimd.affine_select(out=ident[:], in_=ident[:], compare_op=ALU.not_equal, fill=1.0, base=0,
                                    pattern=[[-1, P]], channel_multiplier=1).then_inc(ident_ready, 1)

            def body(turn, steps):
                for s in range(steps):
                    if (e := turn.step(s, 3)) is not None:
                        wait(pool, et_hi_ready, turn.n(1, e + 1))
                        wait(pool, h_done, turn.n(1, e + 1 - RING))
                        nc.gpsimd.tensor_tensor(et_lo[e % RING][:], weight[e % RING][:], et_hi[e % RING][:].bitcast(f32),
                                                ALU.subtract).then_inc(et_lo_ready, 1)
                    if (c := turn.block(s, 11)) is not None:
                        pool.wait_ge(pg_copied, turn.blocks(1, c + 1))
                        wait(pool, mixed, turn.blocks(LINKS, (c - 1) * LINKS + 6))
                        nc.gpsimd.tensor_tensor(pg_b[:], pg[:, :, 0:D], b_bc[:].rearrange("p (u d) -> p u d", u=1).broadcast_to((P, RC, D)),
                                                ALU.add).then_inc(b_added, 1)
                    part, rc = s % ADDS, s // ADDS % RC
                    rc = 1 - rc
                    if (c := turn.block(s, ADDS * (rc + 1) + part)) is not None:
                        wait(pool, counted, turn.blocks(RC, c * RC + rc + 1))
                        cols = slice(C // ADDS * part, C // ADDS * (part + 1))
                        src = adj_n[c % 2][:, rc, :].rearrange("p (r c) -> p c r", c=C)[:, cols, :]
                        nc.gpsimd.tensor_tensor(bias_t[rc][:, cols, :], bias_t[rc][:, cols, :], src, ALU.add).then_inc(bias_added, 1)

            turns(pool, body)

        @block.tensor
        def _(pe):
            pe.wait_ge(ident_ready, 2)
            slot = 0

            def take():
                nonlocal slot
                if slot >= 4:
                    pe.wait_ge(slot_free, slot - 3)
                slot += 1
                return slot_bank[slot - 1]

            for kt, rc, ch in xt_order():
                pe.wait_ge(in_x[2 * rc + ch], 16)
                b = take()
                for i in range(4):
                    last = nc.tensor.transpose(b[:, i * P:(i + 1) * P], xn[:, rc, 4 * ch + i, kt * P:(kt + 1) * P], ident[:])
                last.then_inc(slot_full, 1)
            def three(o, a_hi, a_lo, b_hi, b_lo, start, stop):
                nc.tensor.matmul(o, a_hi, b_hi, start=start, stop=False)
                nc.tensor.matmul(o, a_hi, b_lo, start=False, stop=False)
                return nc.tensor.matmul(o, a_lo, b_hi, start=False, stop=stop)

            pe.wait_ge(slot_free, XT_SLOTS)
            for j in range(NT):
                for which in range(2):
                    if j == 0:
                        pe.wait_ge(proj_split, KT * (which + 1))
                    b = take()
                    for kt in range(KT):
                        cols, out = slice(j * P, (j + 1) * P), slice(which * GW, (which + 1) * GW)
                        last = three(b[:, 0:GW], xt_hi[:, kt, cols], xt_lo[:, kt, cols], proj_hi[:, kt, out], proj_lo[:, kt, out], kt == 0, kt == KT - 1)
                    last.then_inc(slot_full, 1)
            pe.wait_ge(proj_split, 2 * KT + 1)
            for q in range(QCH):
                b = take()
                for kt in range(KT):
                    cols = slice(q * BANK, (q + 1) * BANK)
                    last = three(b[:], wl_hi[:, kt, :], wl_lo[:, kt, :], xt_hi[:, kt, cols], xt_lo[:, kt, cols],
                                 kt == 0, kt == KT - 1)
                last.then_inc(slot_full, 1)
            pe.wait_ge(gate_ready, 2 * NT + 1)

            def products(s, acc, t_hi, t_lo, m_hi, m_lo, done):
                jp = s % JP
                for jj in range(2):
                    j = 2 * jp + jj
                    for rc in range(RC):
                        o, rows = bank[acc + rc][:, 0:GW], slice(rc * P, (rc + 1) * P)
                        first, end = jp == 0 and jj == 0, jp == JP - 1 and jj == 1
                        nc.tensor.matmul(o, t_hi[s % RING][:, jj, rows], m_hi[:, j, :], start=first, stop=False)
                        nc.tensor.matmul(o, t_hi[s % RING][:, jj, rows], m_lo[:, j, :], start=False, stop=False)
                        last = nc.tensor.matmul(o, t_lo[s % RING][:, jj, rows], m_hi[:, j, :], start=False, stop=end)
                last.then_inc(done, 1)

            def body(turn, steps):
                for s in range(steps):
                    if (t := turn.step(s, 0)) is not None:
                        par, jp = divmod(t, JP)
                        if jp == 0:
                            pe.wait_ge(adj_in[par], turn.it * 16 + 16)
                        if turn.kind == "first" and t < 4:
                            pe.wait_ge(slot_free, SLOTS - 3 + t)
                        wait(pe, e_masked, turn.n(1, t - 3))
                        for jj in range(2):
                            for rc in range(RC):
                                j = 2 * jp + jj
                                last = nc.tensor.transpose(bank[4 + t % 4][:, (jj * RC + rc) * P:(jj * RC + rc + 1) * P],
                                                           adj_n[par][:, rc, j * P:(j + 1) * P], ident[:])
                        last.then_inc(t_full, 1)
                    if (t := turn.step(s, 2)) is not None:
                        wait(pe, at_lo_ready, turn.n(1, t + 1))
                        if t % JP == 0:
                            wait(pe, pg_copied, turn.blocks(1, t // JP))
                        products(t, 0, at_hi, at_lo, g_hi, g_lo, g_done)
                    if (t := turn.step(s, 5)) is not None:
                        wait(pe, et_lo_ready, turn.n(1, t + 1))
                        if t % JP == 0:
                            wait(pe, ph_copied, turn.blocks(1, t // JP))
                        products(t, 2, et_hi, et_lo, h_hi, h_lo, h_done)

            turns(pe, body)

            pe.wait_ge(e_masked, C * JP)
            pe.wait_ge(pg_copied, C)
            pe.wait_ge(ph_copied, C)
            for blocks in ([0, 1, 2, 3], [4, 5, 6], [7]):
                pe.wait_ge(x1_ready, blocks[-1] + 1)
                for n, (kt, rc, ch) in enumerate(x1t_order()):
                    for i in range(4):
                        if 4 * ch + i in blocks:
                            last = nc.tensor.transpose(x1t_bank(n)[:, i * P:(i + 1) * P], xn[:, rc, 4 * ch + i, kt * P:(kt + 1) * P], ident[:])
                    if ch == blocks[-1] // 4 and blocks[-1] % 4 == 3:
                        last.then_inc(x1t_full, 1)

        @block.scalar
        def _(act):
            xv = g["x"].rearrange("(rc p c) d -> p rc c d", rc=RC, p=P)
            for i in (1, 3):
                rc, ch = divmod(i, 2)
                act.dma_start(xn[:, rc, 4 * ch:4 * ch + 4, :], xv[:, rc, 4 * ch:4 * ch + 4, :]).then_inc(in_x[i], 16)
            act.dma_start(a_bc[:], g["a_sa"].partition_broadcast(P)).then_inc(in_small, 16)
            for i, w in enumerate((g["wa"], g["wb"])):
                col = w.rearrange("o (s k p) -> p s k o", s=2, p=P)
                act.dma_start(proj[:, :, D + i:D + i + 1], col[:, 0], allow_slow_non_contiguous=True).then_inc(in_small, 16)
                act.dma_start(gate_w[:, i, :], w[:, D:2 * D].partition_broadcast(P)).then_inc(in_small, 16)
            act.dma_start(b_bc[:], g["b_gcnb"].partition_broadcast(P)).then_inc(in_small, 16)
            for i, b in enumerate((g["ba"], g["bb"])):
                act.dma_start(gate_b[:, i:i + 1], b.partition_broadcast(P)).then_inc(in_small, 16)
            for s, (kt, rc, ch) in enumerate(xt_order()):
                act.wait_ge(slot_full, s + 1)
                nc.scalar.copy(xt_dst(xt_hi, kt, rc, ch), slot_bank[s][:].rearrange("x (c p) -> x c p", c=4)).then_inc(slot_hi, 1)
            act.wait_ge(in_w, 32)
            act.wait_ge(in_small, 128)
            for i in range(2 * KT):
                which, kt = divmod(i, KT)
                if i == KT:
                    act.wait_ge(wl_ready, 2 * KT)
                    act.wait_ge(zeroed, 1)
                cols = slice(which * GW, (which + 1) * GW)
                nc.scalar.copy(proj_hi[:, kt, cols], proj[:, kt, cols]).then_inc(proj_hi_ready, 1)
            act.wait_ge(wl_done, KT)
            nc.scalar.copy(wl_hi[:], wl_rep[:]).then_inc(proj_hi_ready, 1)
            for s in range(PROJ0, LEFT0):
                j, which = divmod(s - PROJ0, 2)
                act.wait_ge(slot_full, s + 1)
                if which == 0:
                    nc.scalar.copy(g_hi[:, j, :], slot_bank[s][:, 0:GW]).then_inc(slot_hi, 1)
                else:
                    nc.scalar.copy(h_hi[:, j, 0:D], slot_bank[s][:, 0:D]).then_inc(slot_hi, 1)

            def body(turn, steps):
                def mixed_at(c, k):
                    return turn.blocks(LINKS, c * LINKS + k)

                for s in range(steps):
                    if (c := turn.block(s, 13)) is not None:
                        act.wait_ge(h_done, turn.n(1, (c + 1) * JP))
                        wait(act, mixed, mixed_at(c - 1, 6))
                        nc.scalar.copy(ph[:, 0, :], bank[2][:, 0:GW])
                        nc.scalar.copy(ph[:, 1, :], bank[3][:, 0:GW]).then_inc(ph_copied, 1)
                    if (c := turn.block(s, 15)) is not None:
                        act.wait_ge(mixed, mixed_at(c, 1))
                        nc.scalar.activation(gates[:, 1], gates[:, 0], ACT.Tanh, scale=0.5).then_inc(gate_tanh, 1)
                    if (c := turn.block(s, 17)) is not None:
                        act.wait_ge(mixed, mixed_at(c, 5))
                        for rc in range(RC):
                            last = nc.scalar.activation(ph[:, rc, 0:D], ph[:, rc, 0:D], ACT.Copy, scale=gates[:, 0, rc, 0:1])
                        last.then_inc(ph_scaled, 1)
                    if (c := turn.block(s, 19)) is not None:
                        act.wait_ge(mixed, mixed_at(c, 6))
                        nc.scalar.activation(mix[:], mix[:], ACT.Tanh, scale=0.5).then_inc(mix_act, 1)
                        act.wait_ge(mix_act, turn.blocks(2, 2 * c + 1))
                        nc.scalar.activation(mix[:], mix[:], ACT.Copy, scale=0.5, bias=0.5).then_inc(mix_act, 1)
                    if (c := turn.block(s, 22)) is not None:
                        act.wait_ge(mixed, mixed_at(c, 10))
                        nc.scalar.activation(rstd[:, 1, :], rstd[:, 0, :], ACT.Sqrt).then_inc(std_ready, 1)
                    if (e := turn.step(s, 1)) is not None:
                        wait(act, leaky_ready, turn.n(1, e + 1))
                        nc.scalar.activation(edge[e % RING][:], edge[e % RING][:], ACT.Exp, scale=-1.0).then_inc(exp_ready, 1)
                    if (e := turn.step(s, 3)) is not None:
                        wait(act, e_masked, turn.n(1, e + 1))
                        wait(act, h_done, turn.n(1, e + 1 - RING))
                        nc.scalar.copy(et_hi[e % RING][:], weight[e % RING][:]).then_inc(et_hi_ready, 1)
                    if (t := turn.step(s, 0)) is not None:
                        act.wait_ge(t_full, turn.n(1, t + 1))
                        wait(act, g_done, turn.n(1, t + 1 - RING))
                        nc.scalar.copy(at_hi[t % RING][:], bank[4 + t % 4][:].rearrange("p (j i) -> p j i", j=2)).then_inc(at_hi_ready, 1)
                    if (c := turn.block(s, 9)) is not None:
                        act.wait_ge(g_done, turn.n(1, (c + 1) * JP))
                        wait(act, mixed, mixed_at(c - 1, 1))
                        wait(act, b_added, turn.blocks(1, c))
                        nc.scalar.copy(pg[:, 0, :], bank[0][:, 0:GW])
                        nc.scalar.copy(pg[:, 1, :], bank[1][:, 0:GW]).then_inc(pg_copied, 1)
                    for rc, at in ((0, 3), (1, 7)):
                        if (c := turn.block(s, at)) is not None:
                            act.wait_ge(mask_ready, turn.blocks(RC, c * RC + rc + 1))
                            tile = turn.it * (2 * RC) + c * RC + rc
                            nc.scalar.activation(count_junk[:], bias_t[rc][:].rearrange("p c r -> p (c r)"), ACT.Copy, scale=-1.0 / BIG,
                                                 accum_out=masked_count[:, bass.ds(tile, 1)]).then_inc(counted, 1)
                            act.wait_ge(counted, turn.blocks(RC, c * RC + rc + 1))

            turns(act, body)

            for n in range(0, XT_SLOTS, 2):
                act.wait_ge(x1t_full, n + 1)
                nc.scalar.copy(xt_dst(xt, *x1t_order()[n]), x1t_bank(n)[:].rearrange("x (c p) -> x c p", c=4)).then_inc(x1t_ready, 1)

        @block.vector
        def _(dve):
            nc.vector.memset(ones[:], 1.0)
            nc.vector.memset(h_lo[:, :, D:GW].bitcast(f32), 0.0)
            nc.vector.memset(h_hi[:, :, D + 1:GW].bitcast(f32), 0.0)
            nc.vector.memset(h_hi[:, :, D:D + 1].bitcast(f32), 1.0)
            nc.vector.memset(proj[:, :, GW + HW - 1:GW + HW], 0.0).then_inc(zeroed, 1)
            for s, (kt, rc, ch) in enumerate(xt_order()):
                dve.wait_ge(slot_hi, s + 1)
                nc.vector.tensor_tensor(xt_dst(xt_lo, kt, rc, ch), slot_bank[s][:].rearrange("x (c p) -> x c p", c=4),
                                        xt_dst(xt_hi, kt, rc, ch).bitcast(f32), ALU.subtract).then_inc(slot_free, 1)
            dve.wait_ge(in_w, 32)
            dve.wait_ge(in_small, 128)
            for kt in range(KT):
                for o, dst in ((0, wl[:, kt, :]), (D, proj[:, kt, GW + D:GW + D + 1])):
                    nc.vector.tensor_tensor_reduce(out=junk[:], in0=proj[:, kt, GW:GW + D], in1=a_bc[:, o:o + D], scale=1.0,
                                                   scalar=0.0, op0=ALU.mult, op1=ALU.add, accum_out=dst).then_inc(wl_ready, 1)
                    dve.wait_ge(wl_ready, 2 * kt + (o > 0) + 1)
            for kt in range(KT):
                nc.vector.tensor_scalar(wl_rep[:, kt, :], ones[:], wl[:, kt, :], None, ALU.mult).then_inc(wl_done, 1)
            for i in range(2 * KT):
                which, kt = divmod(i, KT)
                dve.wait_ge(proj_hi_ready, i + 1)
                cols = slice(which * GW, (which + 1) * GW)
                nc.vector.tensor_tensor(proj_lo[:, kt, cols], proj[:, kt, cols], proj_hi[:, kt, cols].bitcast(f32),
                                        ALU.subtract).then_inc(proj_split, 1)
            dve.wait_ge(proj_hi_ready, 2 * KT + 1)
            nc.vector.tensor_tensor(wl_lo[:], wl_rep[:], wl_hi[:].bitcast(f32),
                                    ALU.subtract).then_inc(proj_split, 1)
            for s in range(PROJ0, LEFT0):
                j, which = divmod(s - PROJ0, 2)
                dve.wait_ge(slot_hi, s + 1)
                if which == 0:
                    nc.vector.tensor_tensor(g_lo[:, j, :], slot_bank[s][:, 0:GW], g_hi[:, j, :].bitcast(f32), ALU.subtract).then_inc(slot_free, 1)
                else:
                    nc.vector.tensor_copy(s_right[:, j:j + 1], slot_bank[s][:, D:D + 1])
                    nc.vector.tensor_tensor(h_lo[:, j, 0:D], slot_bank[s][:, 0:D], h_hi[:, j, 0:D].bitcast(f32), ALU.subtract).then_inc(slot_free, 1)
                if s > PROJ0:
                    dve.wait_ge(gate_ready, s - PROJ0)
                nc.vector.tensor_tensor_reduce(out=junk[:], in0=xn[:, j % RC, j // RC, :], in1=gate_w[:, which, :], scale=1.0, scalar=0.0,
                                               op0=ALU.mult, op1=ALU.add, accum_out=gate_xi[:, j, which:which + 1]).then_inc(gate_ready, 1)
            dve.wait_ge(gate_ready, 2 * NT)
            nc.vector.tensor_tensor(gate_xi[:], gate_xi[:], gate_b[:].rearrange("p (u o) -> p u o", u=1).broadcast_to((P, NT, 2)),
                                    ALU.add).then_inc(gate_ready, 1)
            dve.wait_ge(slot_full, SLOTS)
            for q in range(QCH):
                rc, half = divmod(q, 2)
                nc.vector.tensor_copy(s_left[:, :, rc, half * 64:half * 64 + 64],
                                      slot_bank[LEFT0 + q][:].rearrange("x (p c) -> x c p", c=C)).then_inc(slot_free, 1)
            dve.wait_ge(slot_free, SLOTS)
            dve.wait_ge(gate_ready, 2 * NT + 1)
            dve.wait_ge(proj_split, 2 * KT + 1)

            def body(turn, steps):
                def score(t):
                    par, jp = divmod(t, JP)
                    wait(dve, e_masked, turn.n(1, t + 1 - RING))
                    for jj in range(2):
                        j = 2 * jp + jj
                        row = s_left[:, bass.ds(turn.it * 2 + par, 1)].rearrange("x o r p -> x (o r p)")
                        last = nc.vector.tensor_scalar(edge[t % RING][:, jj, :], row, s_right[:, j:j + 1], LEAST, ALU.add, ALU.max)
                    last.then_inc(z_ready, 1)

                def leaky(t):
                    dve.wait_ge(z_ready, turn.n(1, t + 1))
                    nc.vector.scalar_tensor_tensor(out=edge[t % RING][:], in0=edge[t % RING][:], scalar=0.01, in1=edge[t % RING][:],
                                                   op0=ALU.mult, op1=ALU.max).then_inc(leaky_ready, 1)

                def transposed(t):
                    return bank[4 + t % 4][:].rearrange("p (j i) -> p j i", j=2)

                def adjacency_lo(t):
                    wait(dve, at_hi_ready, turn.n(1, t + 1))
                    nc.vector.tensor_tensor(at_lo[t % RING][:], transposed(t), at_hi[t % RING][:].bitcast(f32),
                                            ALU.subtract).then_inc(at_lo_ready, 1)

                def edge_mask(t):
                    wait(dve, exp_ready, turn.n(1, t + 1))
                    wait(dve, et_lo_ready, turn.n(1, t + 1 - RING))
                    nc.vector.scalar_tensor_tensor(out=weight[t % RING][:], in0=transposed(t), scalar=0.0, in1=edge[t % RING][:],
                                                   op0=ALU.not_equal, op1=ALU.mult).then_inc(e_masked, 1)

                def mask(c, rc):
                    dve.wait_ge(adj_in[c % 2], turn.it * 16 + 16)
                    wait(dve, bias_stored[rc], turn.blocks(16, 16 * c))
                    src = adj_n[c % 2][:, rc, :].rearrange("p (r c) -> p c r", c=C)
                    nc.vector.tensor_scalar(bias_t[rc][:], src, 0.0, -BIG, ALU.is_equal, ALU.mult).then_inc(mask_ready, 1)

                def epilogue(c, link):
                    t0 = turn.it * 4 + c * 2

                    def made(k):
                        dve.wait_ge(mixed, turn.blocks(LINKS, c * LINKS + k))

                    if link == 0:
                        dve.wait_ge(pg_copied, turn.blocks(1, c + 1))
                        last = nc.vector.tensor_tensor(gates[:, 0], pg[:, :, D:D + 2], gate_xi[:, bass.ds(t0, 2), :], ALU.add)
                    if link == 1:
                        dve.wait_ge(ph_copied, turn.blocks(1, c + 1))
                        last = nc.vector.tensor_scalar(den[:, 0, :].rearrange("p (r o) -> p r o", o=1), ph[:, :, D:D + 1], 1e-5, None, ALU.add)
                    if link == 2:
                        made(2)
                        last = nc.vector.reciprocal(den[:, 1, :], den[:, 0, :])
                    if link == 3:
                        dve.wait_ge(gate_tanh, turn.blocks(1, c + 1))
                        last = nc.vector.tensor_scalar(gates[:, 2], gates[:, 1], 0.5, 0.5, ALU.mult, ALU.add)
                    if link == 4:
                        made(4)
                        last = nc.vector.tensor_tensor(gates[:, 0, :, 0:1], gates[:, 2, :, 0:1], den[:, 1, :].rearrange("p (r o) -> p r o", o=1), ALU.mult)
                    if link == 5:
                        dve.wait_ge(ph_scaled, turn.blocks(1, c + 1))
                        dve.wait_ge(b_added, turn.blocks(1, c + 1))
                        wait(dve, x1_ready, turn.blocks(1, c))
                        for rc in range(RC):
                            last = nc.vector.scalar_tensor_tensor(out=mix[:, rc, :], in0=pg_b[:, rc, :], scalar=gates[:, 2, rc, 1:2],
                                                                  in1=ph[:, rc, 0:D], op0=ALU.mult, op1=ALU.add)
                    if link == 6:
                        dve.wait_ge(mix_act, turn.blocks(2, 2 * (c + 1)))
                        xc = xn[:, :, bass.ds(turn.it * 2 + c, 1), :].rearrange("p r o d -> p r (o d)")
                        last = nc.vector.tensor_tensor(mix[:], mix[:], xc, ALU.add)
                    if link == 7:
                        made(7)
                        dve.sem_inc(dve_tick)
                        for rc in range(RC):
                            last = nc.vector.bn_stats(stats[:, rc, :], mix[:, rc, :])
                    if link == 8:
                        made(8)
                        dve.sem_inc(dve_tick)
                        for rc in range(RC):
                            last = nc.vector.bn_aggr(moments[:, rc, :], stats[:, rc, :])
                    if link == 9:
                        made(9)
                        last = nc.vector.tensor_scalar(rstd[:, 0, :].rearrange("p (r o) -> p r o", o=1), moments[:, :, 1:2], g["LN_EPS"], None, ALU.add)
                    if link == 10:
                        dve.wait_ge(std_ready, turn.blocks(1, c + 1))
                        last = nc.vector.reciprocal(rstd[:, 2, :], rstd[:, 1, :])
                    last.then_inc(mixed if link < LINKS else rstd_ready, 1)

                def normalize(c):
                    dve.wait_ge(rstd_ready, turn.blocks(1, c + 1))
                    for rc in range(RC):
                        row = xn[:, rc, bass.ds(turn.it * 2 + c, 1), :].rearrange("p o d -> p (o d)")
                        last = nc.vector.tensor_scalar(row, mix[:, rc, :], moments[:, rc, 0:1], rstd[:, 2, rc:rc + 1],
                                                       ALU.subtract, ALU.mult)
                    last.then_inc(x1_ready, 1)

                def links(s, at, *which):
                    if (c := turn.block(s, at)) is not None:
                        for link in which:
                            epilogue(c, link)

                for s in range(steps):
                    links(s, 23, 10)
                    if (t := turn.step(s, 0)) is not None:
                        score(t)
                    links(s, 15, 2)
                    links(s, 21, 7)
                    if (t := turn.step(s, 2)) is not None:
                        edge_mask(t)
                    links(s, 16, 3)
                    links(s, 21, 8)
                    if (c := turn.block(s, 23)) is not None:
                        normalize(c)
                    if (t := turn.step(s, 1)) is not None:
                        adjacency_lo(t)
                    links(s, 14, 0, 1)
                    links(s, 16, 4)
                    links(s, 18, 5)
                    links(s, 20, 6)
                    links(s, 21, 9)
                    if (t := turn.step(s, 0)) is not None:
                        leaky(t)
                    for rc, at in ((0, 2), (1, 6)):
                        if (c := turn.block(s, at)) is not None:
                            mask(c, rc)

            turns(dve, body)

            for n in range(1, XT_SLOTS, 2):
                dve.wait_ge(x1t_full, n + 1)
                nc.vector.tensor_copy(xt_dst(xt, *x1t_order()[n]), x1t_bank(n)[:].rearrange("x (c p) -> x c p", c=4)).then_inc(x1t_ready, 1)


def layer1(nc, g):
    f32, f32r, ALU, ACT, AX = g["f32"], g["f32r"], g["ALU"], g["ACT"], g["AX"]
    N, D, HEADS, C, R, RC, KT, NT = (g[k] for k in ("N", "D", "HEADS", "C", "R", "RC", "KT", "NT"))
    bank, ident, masked_count, xt, w_raw = g["bank"], g["ident"], g["masked_count"], g["xt"], g["w_raw"]
    y = g["x1"]
    NB = N // BANK
    TPB = BANK // P
    QCH = N // BANK
    CH = D * C // BANK
    PROBS = TPB + 1
    RING = 3
    HALF_SCALE = D ** -0.5 / 2

    PROJ = 2 * CH
    SLOTS_H = 3 * PROJ + NT * QCH + NB * TPB // 2
    SPLITS_H = 3 * CH
    HALF = KT // 2

    ctx = ExitStack()
    with ctx:
        def sb(name, shape, dt=f32):
            return ctx.enter_context(nc.sbuf_tensor("l1_" + name, shape, dt))

        def sem(name):
            return ctx.enter_context(nc.semaphore("l1_" + name))

        kt_hi, kt_lo = sb("kt_hi", [P, KT, N], f32r), sb("kt_lo", [P, KT, N], f32r)
        v_hi, v_lo = sb("v_hi", [P, NT, D], f32r), sb("v_lo", [P, NT, D], f32r)
        qt_hi, qt_lo = sb("qt_hi", [P, KT, BANK], f32r), sb("qt_lo", [P, KT, BANK], f32r)
        probs = [sb(f"probs{i}", [P, N])[:] if i < PROBS - KT else xt[:, i - (PROBS - KT), :] for i in range(PROBS)]
        pt_hi, pt_lo = ([sb(f"pt_{w}{i}", [P, BANK], f32r) for i in range(RING)] for w in ("hi", "lo"))
        ot_hi, ot_lo = sb("ot_hi", [P, KT, BANK], f32r), sb("ot_lo", [P, KT, BANK], f32r)
        w_hi, w_lo = ([sb(f"w_{w}{i}", [P, KT, BANK], f32r) for i in range(2)] for w in ("hi", "lo"))
        xh_raw, xh_hi, xh_lo = sb("xh_raw", [P, KT, R]), sb("xh_hi", [P, KT, R], f32r), sb("xh_lo", [P, KT, R], f32r)
        wo_raw, wo_hi, wo_lo = g["wo_raw"], sb("wo_hi", [P, KT, D], f32r), sb("wo_lo", [P, KT, D], f32r)
        bias_t = [sb(f"bias_t{i}", [P, N]) for i in range(2)]
        maxes = sb("maxes", [P, NT, QCH + 1])
        row_max = sb("row_max", [P, NT, 1])
        exp_bias = sb("exp_bias", [P, NT])
        den = sb("den", [P, NT])
        capped, masked_exp, masked_sum, rden = (sb(n, [P, NT]) for n in ("capped", "masked_exp", "masked_sum", "rden"))
        ref_mask = sb("ref_mask", [P, 1])
        stats = sb("stats", [P, NT, 6])
        mv = sb("mv", [P, NT, 2])
        rstd = sb("rstd", [P, 3, NT])

        pool_tick, dve_tick = sem("pool_tick"), sem("dve_tick")
        x1t_stored, ready, w_in, x_in, wo_in = sem("x1t_stored"), sem("ready"), [sem("w_in0"), sem("w_in1")], sem("xh_in"), sem("wo_in")
        bias_in = [sem("bias_in0"), sem("bias_in1")]
        w_hi_ready, w_hi_dve, w_split, w_split_pool = sem("w_hi_ready"), sem("w_hi_dve"), sem("w_split"), sem("w_split_pool")
        xh_hi_ready, xh_split, wo_hi_ready, wo_split = sem("xh_hi_ready"), sem("xh_split"), sem("wo_hi_ready"), sem("wo_split")
        slot_full, slot_hi, slot_free = sem("slot_full"), sem("slot_hi"), sem("slot_free")
        max_ready, scores_ready, probs_ready = sem("max_ready"), sem("scores_ready"), sem("probs_ready")
        pt_full, pt_hi_ready, pt_split, pt_used = sem("pt_full"), sem("pt_hi_ready"), sem("pt_split"), sem("pt_used")
        ot_full, ot_hi_ready, ot_split = sem("ot_full"), sem("ot_hi_ready"), sem("ot_split")
        capped_ready, masked_ready, den_step = sem("capped_ready"), sem("masked_ready"), sem("den_step")
        floor_step, norm_step = sem("floor_step"), sem("norm_step")
        ref_ready, var_ready, std_ready, normed, out_done = (
            sem("ref_ready"), sem("var_ready"), sem("std_ready"), sem("normed"), sem("out_done"))

        class Walk:
            PER_HEAD = dict(slot=SLOTS_H, proj=3 * PROJ, split=SPLITS_H, used=SPLITS_H, rows=1, head=1, tile=NT, block=NB, pt=NB * NT)

            def __init__(self):
                self.n = dict.fromkeys(self.PER_HEAD, 0)
                self.it = None
                self.out_slot = 0

            def at(self, what, k=0):
                here = self.n[what] + k
                return here if self.it is None else self.it * self.PER_HEAD[what] + here

            def past(self, what, k=1):
                self.n[what] += k

        def chunk_waits(w, eng, i):
            loads = 16 * (i // 2)
            if w.it is None and i < 2:
                eng.wait_ge(g["w_first"][i], 16)
            else:
                eng.wait_ge(w_in[i % 2], loads if w.it is None else w.it * (8 * SPLITS_H) + loads)
            if w.it is not None or w.n["slot"]:
                eng.wait_ge(slot_full, w.at("slot"))

        def walk_heads(w, eng, start, rest, end):
            start()
            before = dict(w.n)
            with eng.Fori(0, HEADS - 1) as it:
                w.it = it
                rest()
            w.it = None
            for k, per in w.PER_HEAD.items():
                made = w.n[k] - before[k]
                assert made in (0, per), (k, made, per)
                w.n[k] += (HEADS - 2) * made
            w.out_slot += (HEADS - 2) * SLOTS_H
            end()

        def order(do, first):
            if first:
                do.rows()
                do.split()
                do.split()
            for j in range(CH):
                do.project("k", j)
                do.split()
            if not first:
                do.lead(NB - 1)
            do.project("q", 0)
            do.split()
            if not first:
                do.attend(NB - 1)
            do.scores(0, 0)
            if not first:
                do.project_out(NB - 1)
            do.out_weights()
            for t in range(1, TPB):
                do.scores(0, t)
            do.project("q", 1)
            do.split()
            for j in range(CH):
                do.project("v", j)
                do.split()
            for nb in range(1, NB):
                do.scores(nb, 0)
                do.attend(nb - 1)
                do.scores(nb, 1)
                if nb > 1:
                    do.split()
                do.scores(nb, 2)
                if nb == NB - 1:
                    do.rows()
                do.scores(nb, 3)
                if nb + 1 < NB:
                    do.project("q", nb + 1)
                do.project_out(nb - 1)

        EARLY = list(range((NB - 1) * TPB))
        LATE = list(range((NB - 1) * TPB, NT))

        def last_part(do):
            do.norm_early = True
            do.lead(NB - 1)
            do.attend(NB - 1)
            do.project_out(NB - 1)

        WEIGHTS = ["k"] * CH + ["q"] * 2 + ["v"] * CH + ["q"] * 2
        CHUNK = list(range(CH)) + [0, 1] + list(range(CH)) + [2, 3]
        src_of = {"k": g["wk"], "q": g["wq"], "v": g["wv"]}

        block = ctx.enter_context(nc.Block())

        @block.gpsimd
        def _(pool):
            def lo_half(i, split):
                pool.wait_ge(w_hi_ready, split)
                nc.gpsimd.tensor_tensor(w_lo[i % 2][:, HALF:, :], w_raw[i % 2][:, HALF:, :], w_hi[i % 2][:, HALF:, :].bitcast(f32),
                                        ALU.subtract).then_inc(w_split_pool, 1)

            def load_w(i, split):
                v = src_of[WEIGHTS[i % SPLITS_H]].rearrange("(k p) n -> p k n", p=P)
                chunk = CHUNK[i % SPLITS_H]
                pool.wait_ge(w_split, split)
                pool.wait_ge(w_split_pool, split)
                pool.sem_inc(pool_tick)
                pool.dma_start(w_raw[i % 2][:], v[:, :, chunk * BANK:(chunk + 1) * BANK]).then_inc(w_in[i % 2], 16)

            def head(h, x_rows, wo_rows):
                for i in range(2, SPLITS_H + 2):
                    lo_half(i, h * SPLITS_H + i + 1)
                    if i < SPLITS_H or wo_rows is not None:
                        load_w(i + 2, h * SPLITS_H + i + 1)
                    if i == 8 and wo_rows is not None:
                        pool.wait_ge(wo_split, h + 1)
                        pool.sem_inc(pool_tick)
                        pool.dma_start(wo_raw[:], g["wout"][wo_rows, :].rearrange("(k p) n -> p k n", p=P)).then_inc(wo_in, 16)
                    if i == 9:
                        pool.wait_ge(x1t_stored, 16)
                        pool.wait_ge(xh_split, h + 1)
                        pool.sem_inc(pool_tick)
                        pool.dma_start(xh_raw[:], g["x1t_d"][:, :, x_rows]).then_inc(x_in, 16)

            for i in range(2):
                lo_half(i, i + 1)
                load_w(i + 2, i + 1)
            with pool.Fori(0, HEADS - 1) as h:
                head(h, bass.ds(h * R + R, R), bass.ds(h * D + D, D))
            head(HEADS - 1, slice(0, R), None)
            pool.wait_ge(x_in, 16 * HEADS)

        @block.sync
        def _(sp):
            for i, chunks in enumerate((2, 4)):
                sp.wait_ge(w_split, chunks)
                sp.dma_start(bias_t[i][:], g["bias_d"][i]).then_inc(bias_in[i], 16)
            sp.wait_ge(w_split, 5)
            sp.dma_start(g["x1t_d"], xt[:]).then_inc(x1t_stored, 16)
            for t in range(2, NT):
                sp.wait_ge(max_ready, t - 1)
                sp.dma_start(bias_t[t % 2][:], g["bias_d"][t]).then_inc(bias_in[t % 2], 16)
            with sp.Fori(1, HEADS) as h:
                for t in range(NT):
                    sp.wait_ge(max_ready, h * NT + t - 1)
                    sp.dma_start(bias_t[t % 2][:], g["bias_d"][t]).then_inc(bias_in[t % 2], 16)
            out_v = g["out"].rearrange("(rc p c) d -> p c rc d", rc=RC, p=P)
            for c in range(C):
                sp.wait_ge(normed, RC * (c + 1))
                sp.dma_start(out_v[:, c], y[:, c * RC:(c + 1) * RC, :]).then_inc(out_done, 16)
            sp.wait_ge(out_done, 16 * C)

        @block.tensor
        def _(pe):
            w = Walk()

            def take():
                if w.it is not None or w.n["slot"] >= 4:
                    pe.wait_ge(slot_free, w.at("slot", -3))
                b = bank[w.n["slot"] % 4]
                w.past("slot")
                return b

            def three(o, a_hi, a_lo, b_hi, b_lo, start, stop):
                nc.tensor.matmul(o, a_hi, b_hi, start=start, stop=False)
                nc.tensor.matmul(o, a_hi, b_lo, start=False, stop=False)
                return nc.tensor.matmul(o, a_lo, b_hi, start=False, stop=stop)

            class Do:
                def rows(self):
                    pass

                def split(self):
                    pass

                def out_weights(self):
                    self.wo_lag = 0

                def project(self, which, j):
                    if which == "k" and j == 0:
                        w.past("head")
                        pe.wait_ge(xh_split, w.at("head"))
                        self.wo_lag = -1
                    wh, wl = w_hi[w.n["used"] % 2], w_lo[w.n["used"] % 2]
                    w.past("used")
                    pe.wait_ge(w_split, w.at("used"))
                    pe.wait_ge(w_split_pool, w.at("used"))
                    for i in range(2):
                        b = take()
                        if which == "v":
                            for k in range(KT):
                                rows = slice(i * P, (i + 1) * P)
                                last = three(b[:], xh_hi[:, k, rows], xh_lo[:, k, rows], wh[:, k, :], wl[:, k, :], k == 0, k == KT - 1)
                        else:
                            for ci in range(2):
                                for k in range(KT):
                                    cols = slice(ci * D + i * P, ci * D + (i + 1) * P)
                                    last = three(b[:, ci * R:(ci + 1) * R], wh[:, k, cols], wl[:, k, cols], xh_hi[:, k, :], xh_lo[:, k, :],
                                                 k == 0, k == KT - 1)
                        last.then_inc(slot_full, 1)
                    if which == "q":
                        self.q_slot = w.n["slot"]

                def scores(self, nb, t):
                    if t == 0:
                        pe.wait_ge(slot_free, w.at("slot", self.q_slot - w.n["slot"]))
                    for q in range(QCH):
                        if t == 0 and nb > 0 and q == QCH - 1:
                            self.lead(nb - 1)
                        b = take()
                        for k in range(KT):
                            rows, keys = slice(t * P, (t + 1) * P), slice(q * BANK, (q + 1) * BANK)
                            last = three(b[:], qt_hi[:, k, rows], qt_lo[:, k, rows], kt_hi[:, k, keys], kt_lo[:, k, keys], k == 0, k == KT - 1)
                        last.then_inc(slot_full, 1)

                def transposes(self, nb, k):
                    if w.it is not None or w.n["pt"] >= 2:
                        pe.wait_ge(pt_split, w.at("pt", -1))
                    for t in range(TPB):
                        last = nc.tensor.transpose(bank[4 + k % 2][:, t * P:(t + 1) * P],
                                                   probs[(nb * TPB + t) % PROBS][:, k * P:(k + 1) * P], ident[:])
                    last.then_inc(pt_full, 1)
                    w.past("pt")

                def lead(self, nb):
                    w.past("block")
                    pe.wait_ge(probs_ready, w.at("block") * TPB)
                    self.transposes(nb, 0)
                    self.transposes(nb, 1)

                def attend(self, nb):
                    for k in range(NT):
                        if k + 2 < NT:
                            self.transposes(nb, k + 2)
                        behind = min(k + 3, NT)
                        pe.wait_ge(pt_split, w.at("pt", k + 1 - behind))
                        if k == 0 and (w.it is not None or w.n["block"] > 1):
                            pe.wait_ge(ot_split, w.at("block", -1))
                        ph, pl = pt_hi[(nb * NT + k) % RING], pt_lo[(nb * NT + k) % RING]
                        for d in range(KT):
                            cols = slice(d * P, (d + 1) * P)
                            last = three(bank[6 + d][:], v_hi[:, k, cols], v_lo[:, k, cols], ph[:], pl[:], k == 0, k == NT - 1)
                        last.then_inc(pt_used, 1)

                def project_out(self, nb):
                    pe.wait_ge(ot_split, w.at("block"))
                    pe.wait_ge(wo_split, w.at("head", self.wo_lag))
                    for pair in range(TPB // 2):
                        b = take()
                        for i in range(2):
                            t = 2 * pair + i
                            for k in range(KT):
                                rows = slice(t * P, (t + 1) * P)
                                last = three(b[:, i * D:(i + 1) * D], ot_hi[:, k, rows], ot_lo[:, k, rows], wo_hi[:, k, :], wo_lo[:, k, :],
                                             k == 0, k == KT - 1)
                        last.then_inc(slot_full, 1)

            do = Do()

            walk_heads(w, pe, lambda: order(do, True), lambda: order(do, False), lambda: last_part(do))

        @block.scalar
        def _(act):
            w = Walk()

            class Do:
                def split(self):
                    i = w.n["split"]
                    w.past("split")
                    chunk_waits(w, act, i)
                    nc.scalar.copy(w_hi[i % 2][:, HALF:, :], w_raw[i % 2][:, HALF:, :]).then_inc(w_hi_ready, 1)
                    self.exponentials_left("split")
                    if self.projected == "v":
                        self.exponentials_left("v")

                def rows(self):
                    w.past("rows")
                    src = xt[:, :, 0:R]
                    if w.it is not None:
                        src = xh_raw[:]
                        act.wait_ge(x_in, 16 * w.at("rows", -1))
                        act.wait_ge(slot_full, w.at("slot"))
                    elif w.n["slot"]:
                        src = xh_raw[:]
                        act.wait_ge(x_in, 16)
                        act.wait_ge(slot_full, w.n["slot"])
                    nc.scalar.copy(xh_hi[:], src).then_inc(xh_hi_ready, 1)
                    self.exponentials_left("rows")

                def out_weights(self):
                    w.past("head")
                    if w.it is None:
                        act.wait_ge(g["wo_first"], 16)
                    else:
                        act.wait_ge(wo_in, 16 * w.at("head", -1))
                        act.wait_ge(slot_full, w.at("slot"))
                    nc.scalar.copy(wo_hi[:], wo_raw[:]).then_inc(wo_hi_ready, 1)

                def project(self, which, j):
                    self.projected = which
                    for i in range(2):
                        b = bank[w.n["slot"] % 4]
                        w.past("slot")
                        w.past("proj")
                        act.wait_ge(slot_full, w.at("slot"))
                        if which == "k":
                            nc.scalar.copy(kt_hi[:, i, j * BANK:(j + 1) * BANK], b[:]).then_inc(slot_hi, 1)
                        elif which == "q":
                            nc.scalar.mul(qt_hi[:, i, :], b[:], HALF_SCALE).then_inc(slot_hi, 1)
                        else:
                            dst = v_hi[:, 4 * j:4 * j + 4, :].rearrange("p (c r) d -> p r c d", r=RC)[:, i]
                            nc.scalar.copy(dst, b[:].rearrange("p (c d) -> p c d", c=2)).then_inc(slot_hi, 1)

                pending = None
                late = None
                projected = None
                norm_early = False

                def standard(self, tiles, part):
                    cols = slice(tiles[0], tiles[-1] + 1)
                    act.wait_ge(var_ready, part)
                    nc.scalar.activation(rstd[:, 1, cols], rstd[:, 0, cols], ACT.Sqrt).then_inc(std_ready, 1)

                def exponentials_left(self, behind):
                    if self.late and self.late[0] == behind:
                        self.exponentials(*self.late[1:])
                        self.late = None

                def scores(self, nb, t):
                    w.past("slot", QCH)
                    w.past("tile")
                    if t == 0 and nb > 0:
                        self.lead(nb - 1)
                        self.pending = (nb, t, w.at("tile"))
                    elif t == TPB - 1:
                        self.late = ("v" if nb == 0 else "out", nb, t, w.at("tile"))
                    elif t == 1 and nb > 1:
                        self.late = ("split", nb, t, w.at("tile"))
                    elif t == 2 and nb == NB - 1:
                        self.late = ("rows", nb, t, w.at("tile"))
                    else:
                        self.exponentials(nb, t, w.at("tile"))

                def exponentials(self, nb, t, tile):
                    n = nb * TPB + t
                    p = probs[n % PROBS]
                    act.wait_ge(scores_ready, tile)
                    nc.scalar.activation(p, p, ACT.Exp, bias=exp_bias[:, n:n + 1], scale=2.0, accum_out=den[:, n:n + 1]).then_inc(probs_ready, 1)

                def transposed(self, nb, k):
                    w.past("pt")
                    act.wait_ge(pt_full, w.at("pt"))
                    if w.it is not None or w.n["pt"] > RING:
                        act.wait_ge(pt_used, w.at("pt", -RING))
                    nc.scalar.copy(pt_hi[(nb * NT + k) % RING][:], bank[4 + k % 2][:]).then_inc(pt_hi_ready, 1)

                def lead(self, nb):
                    w.past("block")
                    self.transposed(nb, 0)
                    self.transposed(nb, 1)

                def attend(self, nb):
                    for k in range(2, NT):
                        self.transposed(nb, k)
                        if k == 2 and self.pending:
                            self.exponentials(*self.pending)
                            self.pending = None
                        if k == 10 and self.norm_early:
                            self.standard(EARLY, 1)
                    act.wait_ge(pt_used, w.at("pt"))
                    if w.it is not None or w.n["block"] > 1:
                        act.wait_ge(slot_full, w.at("slot", w.out_slot - w.n["slot"]))
                    for d in range(KT):
                        nc.scalar.copy(ot_hi[:, d, :], bank[6 + d][:]).then_inc(ot_hi_ready, 1)
                    cols = slice(nb * TPB, (nb + 1) * TPB)
                    act.wait_ge(capped_ready, w.at("block"))
                    nc.scalar.activation(masked_exp[:, cols], capped[:, cols], ACT.Exp, bias=ref_mask[:, 0:1]).then_inc(masked_ready, 1)

                def project_out(self, nb):
                    self.exponentials_left("out")
                    w.past("slot", TPB // 2)
                    w.out_slot = w.n["slot"]

            do = Do()

            act.wait_ge(ready, 1)
            walk_heads(w, act, lambda: order(do, True), lambda: order(do, False), lambda: last_part(do))
            do.standard(LATE, 2)

        @block.vector
        def _(dve):
            w = Walk()

            class Do:
                norm_early = False
                steps = 0

                def lo(self, dst, src, hi):
                    return nc.vector.tensor_tensor(dst, src, hi.bitcast(f32), ALU.subtract)

                def norm_done(self, ins):
                    self.steps += 1
                    ins.then_inc(norm_step, 1)

                def row_stats(self, tiles):
                    dve.wait_ge(slot_free, w.n["slot"])
                    for t in tiles:
                        last = nc.vector.bn_stats(stats[:, t, :], y[:, t, :])
                    self.norm_done(last)

                def row_moments(self, tiles):
                    dve.wait_ge(norm_step, self.steps)
                    for t in tiles:
                        last = nc.vector.bn_aggr(mv[:, t, :], stats[:, t, :])
                    self.norm_done(last)
                    cols = slice(tiles[0], tiles[-1] + 1)
                    dve.wait_ge(norm_step, self.steps)
                    nc.vector.tensor_scalar(rstd[:, 0, cols].rearrange("p (t o) -> p t o", o=1), mv[:, cols, 1:2], g["LN_EPS"], None,
                                            ALU.add).then_inc(var_ready, 1)

                def row_rstd(self, tiles, part):
                    cols = slice(tiles[0], tiles[-1] + 1)
                    dve.wait_ge(std_ready, part)
                    self.norm_done(nc.vector.reciprocal(rstd[:, 2, cols], rstd[:, 1, cols]))

                def normalize(self, tiles):
                    dve.wait_ge(norm_step, self.steps)
                    for t in tiles:
                        nc.vector.tensor_scalar(y[:, t, :], y[:, t, :], mv[:, t, 0:1], rstd[:, 2, t:t + 1], ALU.subtract,
                                                ALU.mult).then_inc(normed, 1)

                def split(self):
                    i = w.n["split"]
                    w.past("split")
                    chunk_waits(w, dve, i)
                    nc.vector.tensor_copy(w_hi[i % 2][:, 0:HALF, :], w_raw[i % 2][:, 0:HALF, :]).then_inc(w_hi_dve, 1)
                    dve.wait_ge(w_hi_dve, w.at("split"))
                    self.lo(w_lo[i % 2][:, 0:HALF, :], w_raw[i % 2][:, 0:HALF, :], w_hi[i % 2][:, 0:HALF, :]).then_inc(w_split, 1)

                def rows(self):
                    w.past("rows")
                    dve.wait_ge(xh_hi_ready, w.at("rows"))
                    first = w.it is None and w.n["rows"] == 1
                    self.lo(xh_lo[:], xt[:, :, 0:R] if first else xh_raw[:], xh_hi[:]).then_inc(xh_split, 1)

                def out_weights(self):
                    w.past("head")
                    dve.wait_ge(wo_hi_ready, w.at("head"))
                    self.lo(wo_lo[:], wo_raw[:], wo_hi[:]).then_inc(wo_split, 1)

                def project(self, which, j):
                    for i in range(2):
                        b = bank[w.n["slot"] % 4]
                        w.past("slot")
                        w.past("proj")
                        dve.wait_ge(slot_hi, w.at("proj"))
                        if which == "k":
                            keys = slice(j * BANK, (j + 1) * BANK)
                            last = self.lo(kt_lo[:, i, keys], b[:], kt_hi[:, i, keys])
                        elif which == "q":
                            last = nc.vector.scalar_tensor_tensor(out=qt_lo[:, i, :], in0=b[:], scalar=HALF_SCALE, in1=qt_hi[:, i, :].bitcast(f32),
                                                                  op0=ALU.mult, op1=ALU.subtract)
                        else:
                            def part(t):
                                return t[:, 4 * j:4 * j + 4, :].rearrange("p (c r) d -> p r c d", r=RC)[:, i]
                            last = self.lo(part(v_lo), b[:].rearrange("p (c d) -> p c d", c=2), part(v_hi))
                        last.then_inc(slot_free, 1)

                def scores(self, nb, t):
                    n = nb * TPB + t
                    w.past("tile")
                    dve.wait_ge(bias_in[n % 2], self.bias_loads(n))
                    if w.it is None and n == PROBS - KT:
                        dve.wait_ge(x1t_stored, 16)
                    if n >= PROBS:
                        dve.wait_ge(pt_full, w.at("pt"))
                    for q in range(QCH):
                        if t == 0 and nb > 0 and q == QCH - 1:
                            self.lead(nb - 1)
                        b = bank[w.n["slot"] % 4]
                        w.past("slot")
                        keys = slice(q * BANK, (q + 1) * BANK)
                        dve.wait_ge(slot_full, w.at("slot"))
                        dve.sem_inc(dve_tick)
                        nc.vector.tensor_tensor_reduce(out=probs[n % PROBS][:, keys], in0=b[:], in1=bias_t[n % 2][:, keys], scale=1.0, scalar=LOWEST,
                                                       op0=ALU.add, op1=ALU.max, accum_out=maxes[:, n, q:q + 1]).then_inc(slot_free, 1)
                    dve.wait_ge(slot_free, w.at("slot"))
                    nc.vector.tensor_reduce(out=row_max[:, n, :], in_=maxes[:, n, :], axis=AX.X, op=ALU.max).then_inc(max_ready, 1)
                    dve.wait_ge(max_ready, w.at("tile"))
                    nc.vector.tensor_scalar(exp_bias[:, n:n + 1], row_max[:, n, :], -2.0, None, ALU.mult).then_inc(scores_ready, 1)
                    if t == TPB - 1:
                        cols = slice(nb * TPB, (nb + 1) * TPB)
                        dve.wait_ge(scores_ready, w.at("tile"))
                        nc.vector.tensor_scalar(capped[:, cols], exp_bias[:, cols], -REF_MASK, None, ALU.min).then_inc(capped_ready, 1)

                def bias_loads(self, n):
                    k = 16 * ((w.n["tile"] - 1) // NT) * (NT // 2) + 16 * (n // 2 + 1)
                    return k if w.it is None else w.it * (8 * NT) + k

                def transposed(self, nb, k):
                    w.past("pt")
                    r = (nb * NT + k) % RING
                    dve.wait_ge(pt_hi_ready, w.at("pt"))
                    self.lo(pt_lo[r][:], bank[4 + k % 2][:], pt_hi[r][:]).then_inc(pt_split, 1)

                def lead(self, nb):
                    w.past("block")
                    self.transposed(nb, 0)
                    self.transposed(nb, 1)

                def attend(self, nb):
                    for k in range(2, NT):
                        self.transposed(nb, k)
                        if self.norm_early:
                            if k in range(2, 8):
                                self.row_stats(EARLY[2 * (k - 2):2 * (k - 1)])
                            if k == 8:
                                self.row_moments(EARLY)
                            if k == 11:
                                self.row_rstd(EARLY, 1)
                            if k in range(12, 16):
                                self.normalize(EARLY[3 * (k - 12):3 * (k - 11)])
                    dve.wait_ge(ot_hi_ready, w.at("block") * KT)
                    for d in range(KT):
                        last = self.lo(ot_lo[:, d, :], bank[6 + d][:], ot_hi[:, d, :])
                    last.then_inc(ot_split, 1)
                    cols = slice(nb * TPB, (nb + 1) * TPB)
                    dve.wait_ge(masked_ready, w.at("block"))
                    nc.vector.tensor_tensor(masked_sum[:, cols], masked_exp[:, cols], masked_count[:, cols], ALU.mult).then_inc(den_step, 1)
                    dve.wait_ge(den_step, w.at("block") * 3 - 2)
                    nc.vector.tensor_tensor(masked_sum[:, cols], masked_sum[:, cols], den[:, cols], ALU.add).then_inc(den_step, 1)
                    dve.wait_ge(den_step, w.at("block") * 3 - 1)
                    nc.vector.reciprocal(rden[:, cols], masked_sum[:, cols]).then_inc(den_step, 1)

                def project_out(self, nb):
                    dve.wait_ge(den_step, w.at("block") * 3)
                    for pair in range(TPB // 2):
                        b = bank[w.n["slot"] % 4]
                        w.past("slot")
                        dve.wait_ge(slot_full, w.at("slot"))
                        for i in range(2):
                            n = nb * TPB + 2 * pair + i
                            last = nc.vector.scalar_tensor_tensor(out=y[:, n, :], in0=b[:, i * D:(i + 1) * D], scalar=rden[:, n:n + 1],
                                                                  in1=y[:, n, :], op0=ALU.mult, op1=ALU.add)
                        last.then_inc(slot_free, 1)

            do = Do()

            nc.vector.memset(ref_mask[:], REF_MASK).then_inc(ref_ready, 1)
            dve.wait_ge(ref_ready, 1)
            floor = maxes[:, :, QCH:QCH + 1]
            nc.vector.tensor_scalar(row_max[:], masked_count[:].rearrange("p (t o) -> p t o", o=1), 0.0, -LOWEST, ALU.is_equal, ALU.mult).then_inc(floor_step, 1)
            dve.wait_ge(floor_step, 1)
            nc.vector.tensor_scalar(floor, row_max[:], -1.0, REF_MASK / 2, ALU.mult, ALU.add).then_inc(ready, 1)
            dve.wait_ge(ready, 1)
            walk_heads(w, dve, lambda: order(do, True), lambda: order(do, False), lambda: last_part(do))

            do.row_stats(LATE)
            do.row_moments(LATE)
            do.row_rstd(LATE, 2)
            do.normalize(LATE)


_INS = ["x", "adj", "L0_gnn_W_sa", "L0_gnn_a_sa", "L0_gnn_W_gcnb", "L0_gnn_b_gcnb", "L0_gnn_Wa", "L0_gnn_ba",
        "L0_gnn_Wb", "L0_gnn_bb", "L1_gnn_Wq", "L1_gnn_Wk", "L1_gnn_Wv", "L1_gnn_Wout"]


def kernel(**inputs):
    import numpy as _np
    import concourse.bacc as _bacc
    from concourse import mybir as _mybir
    from concourse.bass_utils import run_bass_kernel_spmd as _run

    nc = _bacc.Bacc("TRN2", target_bir_lowering=False, num_devices=1)
    arrays, args = {}, []
    for name in _INS:
        a = _np.ascontiguousarray(inputs[name])
        arrays[f"in_{name}_dram"] = a
        args.append(nc.dram_tensor(f"in_{name}_dram", a.shape, _mybir.dt.from_np(a.dtype), kind="ExternalInput").ap())
    args.append(nc.dram_tensor("out_0_dram", (2048, 256), _mybir.dt.float32, kind="ExternalOutput").ap())
    gnn_two_layers(nc, *args)
    r = _run(nc, [arrays], core_ids=[0])
    return r.results[0]["out_0_dram"]
```
